# Optimizing a Trainium2 kernel written in Bass

```python
import numpy as np
import jax
import jax.numpy as jnp

def _softmax(x, axis=-1):
    return jax.nn.softmax(x, axis=axis)

def _gelu(x):
    return jax.nn.gelu(x, approximate=True)

def _silu(x):
    return jax.nn.silu(x)

def _sigmoid(x):
    return jax.nn.sigmoid(x)

def _layernorm(x, axis=-1, eps=1e-05):
    m = jnp.mean(x, axis=axis, keepdims=True)
    v = jnp.var(x, axis=axis, keepdims=True)
    return (x - m) / jnp.sqrt(v + eps)

def _scatter_add(tgt, idx, src, axis=0):
    return tgt.at[idx].add(src)

def _segment_sum(src, seg, n):
    return jax.ops.segment_sum(src, seg, n)
kernel_name = 'mk_flamingo_gated_d1_seqx_r8_15deea'

def setup_inputs(seed: int=0):
    np.random.seed(seed)
    _w = jnp.asarray

    def _rec_inputs():
        import jax
        import jax.numpy as jnp
        _rk = jax.random.key(seed)
        x = -0.0002928 + 1 * jax.random.normal(jax.random.fold_in(_rk, 1), (8, 256, 128), jnp.float32)
        _lenS = 256 - jax.random.randint(jax.random.fold_in(_rk, 7), (8,), 0, max(1, 256 // 4) + 1, jnp.int32)
        _lenS2 = 512 - jax.random.randint(jax.random.fold_in(_rk, 8), (8,), 0, max(1, 512 // 4) + 1, jnp.int32)
        _ctx_1024P = jax.random.normal(jax.random.fold_in(_rk, 11), (8, 16, 128), jnp.float32)
        _ctx_1024c = jax.random.dirichlet(jax.random.fold_in(_rk, 511), 0.3 * jnp.ones((16,), jnp.float32), (8, 512))
        _ctx_1024t = jnp.einsum('bsk,bkd->bsd', _ctx_1024c, _ctx_1024P)
        _ctx_1024t = _ctx_1024t * jax.lax.rsqrt(jnp.mean(jnp.square(_ctx_1024t)) + 1e-12) * 0.953939
        ctx_1024 = -1.39393e-06 + 0.999914 * (_ctx_1024t + 0.3 * jax.random.normal(jax.random.fold_in(_rk, 611), (8, 512, 128), jnp.float32))
        _validS = jnp.arange(256)[None, :] < _lenS[:, None]
        _validS2 = jnp.arange(512)[None, :] < _lenS2[:, None]
        _causal = jnp.tril(jnp.ones((256, 256), dtype=bool))
        mask_BxSxS2_bf0 = jnp.logical_not(jnp.ones((8, 256, 512), dtype=bool))
        _g = jax.random.normal(jax.random.fold_in(_rk, 9001), (2, 1), jnp.float32)
        _g = jnp.sign(_g) * jnp.maximum(jnp.abs(_g), 1.0) + (_g == 0) * 1.0
        g_xattn = _g[0]
        g_ffn = _g[1]
        return (x, ctx_1024, mask_BxSxS2_bf0, g_xattn, g_ffn)
    x, ctx_1024, mask_BxSxS2_bf0, g_xattn, g_ffn = _rec_inputs()

    def _L0_xattn_setup():
        import jax, jax.numpy as jnp
        import numpy as np
        D_MODEL = 128
        NUM_HEADS = 16
        D_K = D_MODEL // NUM_HEADS

        def _split_heads(x):
            B, S, _ = x.shape
            return x.reshape(B, S, NUM_HEADS, D_K).transpose(0, 2, 1, 3)
        key = jax.random.key(seed)
        ks = jax.random.split(key, 8)
        B, S = (2, 256)
        scale = 1.0 / np.sqrt(D_MODEL)
        return {'query': jax.random.normal(ks[0], (B, S, D_MODEL), jnp.float32), 'key': jax.random.normal(ks[1], (B, S, D_MODEL), jnp.float32), 'value': jax.random.normal(ks[2], (B, S, D_MODEL), jnp.float32), 'mask': jnp.zeros((B, S, S), dtype=bool), 'W_Q': jax.random.normal(ks[3], (D_MODEL, D_MODEL), jnp.float32) * scale, 'W_K': jax.random.normal(ks[4], (D_MODEL, D_MODEL), jnp.float32) * scale, 'W_V': jax.random.normal(ks[5], (D_MODEL, D_MODEL), jnp.float32) * scale, 'W_O': jax.random.normal(ks[6], (D_MODEL, D_MODEL), jnp.float32) * scale}
    _L0_xattn_all = _L0_xattn_setup()
    _L0_xattn_in = {k: v for k, v in _L0_xattn_all.items() if k in ('W_Q', 'W_K', 'W_V', 'W_O')}
    del _L0_xattn_all

    def _L0_ffn_setup():
        import jax, jax.numpy as jnp
        import numpy as np
        NUM_EXPERTS = 8
        TOP_K = 2
        key = jax.random.key(seed)
        ks = jax.random.split(key, 6)
        B, S, D, H, E = (4, 128, 128, 256, NUM_EXPERTS)
        x = jax.random.normal(ks[0], (B, S, D), dtype=jnp.float32)
        Wg = jax.random.normal(ks[1], (D, E), dtype=jnp.float32) * 0.02
        W1 = jax.random.normal(ks[2], (E, D, H), dtype=jnp.float32) * 0.02
        b1 = jax.random.normal(ks[3], (E, H), dtype=jnp.float32) * 0.02
        W2 = jax.random.normal(ks[4], (E, H, D), dtype=jnp.float32) * 0.02
        b2 = jax.random.normal(ks[5], (E, D), dtype=jnp.float32) * 0.02
        return {'x': x, 'Wg': Wg, 'W1': W1, 'b1': b1, 'W2': W2, 'b2': b2}
    _L0_ffn_all = _L0_ffn_setup()
    _L0_ffn_in = {k: v for k, v in _L0_ffn_all.items() if k in ('Wg', 'W1', 'b1', 'W2', 'b2')}
    del _L0_ffn_all
    return {'x': x, 'ctx_1024': ctx_1024, 'mask_BxSxS2_bf0': mask_BxSxS2_bf0, 'g_xattn': g_xattn, 'g_ffn': g_ffn, 'L0_xattn_W_Q': _L0_xattn_in['W_Q'], 'L0_xattn_W_K': _L0_xattn_in['W_K'], 'L0_xattn_W_V': _L0_xattn_in['W_V'], 'L0_xattn_W_O': _L0_xattn_in['W_O'], 'L0_ffn_Wg': _L0_ffn_in['Wg'], 'L0_ffn_W1': _L0_ffn_in['W1'], 'L0_ffn_b1': _L0_ffn_in['b1'], 'L0_ffn_W2': _L0_ffn_in['W2'], 'L0_ffn_b2': _L0_ffn_in['b2']}

def reference(x, ctx_1024, mask_BxSxS2_bf0, g_xattn, g_ffn, L0_xattn_W_Q, L0_xattn_W_K, L0_xattn_W_V, L0_xattn_W_O, L0_ffn_Wg, L0_ffn_W1, L0_ffn_b1, L0_ffn_W2, L0_ffn_b2):
    import jax
    import jax.numpy as jnp

    def _L0_xattn_ref(query, key, value, mask, W_Q, W_K, W_V, W_O):
        import jax, jax.numpy as jnp
        import numpy as np
        D_MODEL = 128
        NUM_HEADS = 16
        D_K = D_MODEL // NUM_HEADS

        def _split_heads(x):
            B, S, _ = x.shape
            return x.reshape(B, S, NUM_HEADS, D_K).transpose(0, 2, 1, 3)
        Q = _split_heads(jnp.einsum('bsd,ed->bse', query, W_Q))
        K = _split_heads(jnp.einsum('bsd,ed->bse', key, W_K))
        V = _split_heads(jnp.einsum('bsd,ed->bse', value, W_V))
        scores = jnp.einsum('bhqd,bhkd->bhqk', Q, K) / jnp.sqrt(jnp.float32(D_K))
        m = mask[:, None, :, :]
        scores = jnp.where(m, -jnp.inf, scores)
        attn = jax.nn.softmax(scores, axis=-1)
        attn = jnp.where(jnp.isnan(attn), 0.0, attn)
        out = jnp.einsum('bhqk,bhkd->bhqd', attn, V)
        B, H, S, _ = out.shape
        out = out.transpose(0, 2, 1, 3).reshape(B, S, D_MODEL)
        return jnp.einsum('bsd,ed->bse', out, W_O)

    def _L0_ffn_ref(x, Wg, W1, b1, W2, b2):
        import jax, jax.numpy as jnp
        import numpy as np
        NUM_EXPERTS = 8
        TOP_K = 2
        B, S, D = x.shape
        E, _, H = W1.shape
        OUT = W2.shape[2]
        xm = x.reshape(-1, D)
        logits = xm @ Wg
        probs = jax.nn.softmax(logits, axis=-1)
        topk_p, topk_i = jax.lax.top_k(probs, TOP_K)
        flat_e = topk_i.reshape(-1)
        flat_p = topk_p.reshape(-1)
        order = jnp.argsort(flat_e)
        tok_idx = order // TOP_K
        e_sorted = flat_e[order]
        p_sorted = flat_p[order]
        xs = xm[tok_idx]
        y = jnp.zeros((xs.shape[0], OUT), dtype=xs.dtype)
        for e in range(E):
            h = jax.nn.relu(xs @ W1[e] + b1[e])
            ye = h @ W2[e] + b2[e]
            m = (e_sorted == e)[:, None].astype(xs.dtype)
            y = y + m * ye
        y = y * p_sorted[:, None]
        out = jnp.zeros((B * S, OUT), dtype=y.dtype).at[tok_idx].add(y)
        return out.reshape(B, S, OUT)
    x = x + jnp.tanh(g_xattn[0]) * _L0_xattn_ref(_layernorm(x, axis=-1), ctx_1024, ctx_1024, mask_BxSxS2_bf0, L0_xattn_W_Q, L0_xattn_W_K, L0_xattn_W_V, L0_xattn_W_O)
    x = x + jnp.tanh(g_ffn[0]) * _L0_ffn_ref(_layernorm(x, axis=-1), L0_ffn_Wg, L0_ffn_W1, L0_ffn_b1, L0_ffn_W2, L0_ffn_b2)
    return x

_drawn_inputs = setup_inputs


def setup_inputs(seed=0):
    import zlib

    import numpy as np

    out = dict(_drawn_inputs(seed))
    spreads = {}
    factors = {'L0_ffn_Wg': 5.845,
     'L0_ffn_W1': 6.698,
     'L0_ffn_b1': 8.0,
     'L0_ffn_W2': 5.54,
     'L0_ffn_b2': 8.0}
    for name, (base, spread) in spreads.items():
        noise = np.random.default_rng([zlib.crc32(name.encode()), seed]).standard_normal(out[name].shape)
        drawn = base * np.exp(spread * noise) if base else spread * noise
        out[name] = jnp.asarray(drawn.astype(out[name].dtype))
    for name, factor in factors.items():
        out[name] = (out[name] * factor).astype(out[name].dtype)
    return out
```

```python
from contextlib import ExitStack

import concourse.bass as bass
from concourse import mybir

F32 = mybir.dt.float32
BF16 = mybir.dt.bfloat16
U8 = mybir.dt.uint8
U32 = mybir.dt.uint32
I32 = mybir.dt.int32
ALU = mybir.AluOpType
ACT = mybir.ActivationFunctionType
AX_X = mybir.AxisListType.X

P = 128
B = 8
S = 256
S2 = 512
D = 128
H = 16
DK = D // H
QT = S // P
KC = S2 // P
PAIRS = H // 2
E = 8
HC = 2
VW = 32
UNITS = 2 * PAIRS
GROUPS = 4
SCALE = 1.0 / float(DK) ** 0.5
EPS = 1e-5
MASKED = -1e30
LOWEST = -1e29

K_PARTS = [0, 0, 0, 1, 1, 2]
Q_PARTS = [0, 1, 2, 0, 1, 0]
TERMS = len(K_PARTS)
QK_ROWS = TERMS * DK
M_ROWS = 2
STACK_DMAS = 2 * TERMS * 2
MAX_DMAS = 2

MX_UNITS = [(qt, i) for qt in range(QT) for i in range(PAIRS)]
MX_PER_SLOT = {4: 1, 5: 1, 6: 1, 7: 1, 8: 2, 9: 2, 10: 2, 11: 2, 12: 2, 13: 2}
EXPERT_SLOT = 7
ROUTE_STEPS = 9


def mx_units(slot):
    first = sum(n for s, n in MX_PER_SLOT.items() if s < slot)
    return range(first, first + MX_PER_SLOT.get(slot, 0))


class Batch:

    def __init__(self, r, off):
        self.n = 2 * r + off
        self.turn = r + off // 2
        self.par = off % 2
        self.first = isinstance(self.n, int) and self.n == 0
        self.early = isinstance(self.n, int) and self.n < 2

    def tiles(self):
        return bass.ds(2 * self.n, QT)


def count(batch, per, k):
    return per * batch.n + k


def hold(engine, semaphore, value):
    engine.wait_ge(semaphore, value)
    engine.nop(nofuse=True)


def steps(engine, step):
    step(Batch(0, 1), Batch(0, 0), None, Batch(0, 2))
    step(Batch(0, 2), Batch(0, 1), Batch(0, 0), Batch(0, 3))
    with engine.Fori(0, 2) as r:
        step(Batch(r, 3), Batch(r, 2), Batch(r, 1), Batch(r, 4))
        step(Batch(r, 4), Batch(r, 3), Batch(r, 2), Batch(r, 5))
    step(Batch(0, 7), Batch(0, 6), Batch(0, 5), None)
    step(None, Batch(0, 7), Batch(0, 6), None)
    step(None, None, Batch(0, 7), None)


def build(nc, x, ctxT, mask, gates, wqT, wkT, wvT, woT, wg, w1, b1, w2, b2, eye, out):
    with ExitStack() as stack:
        def sb(name, shape, dt):
            return stack.enter_context(nc.sbuf_tensor(name, shape, dt))

        def sem(name):
            return stack.enter_context(nc.semaphore(name))

        x_all = sb("x_all", [P, B * QT, D], F32)
        mask_all = sb("mask_all", [P, B * QT, S2], U8)
        mask_sb = [sb(f"mask_sb{p}", [P, QT, S2], U8) for p in range(2)]
        ctx_sb = [sb(f"ctx_sb{p}", [P, S2], F32) for p in range(2)]
        maskb = [sb(f"maskb{p}", [P, QT, S2], BF16) for p in range(2)]
        k_stack = [sb(f"k_stack{p}", [P, PAIRS, S2], BF16) for p in range(2)]
        q_stack = [sb(f"q_stack{p}", [P, PAIRS, S], BF16) for p in range(2)]
        v_sb = [sb(f"v_sb{p}", [P, KC, H, VW], F32) for p in range(2)]
        k_parts = sb("k_parts", [P, 3, S2], BF16)
        q_parts = sb("q_parts", [P, 3, S], BF16)
        k_rest = sb("k_rest", [P, S2], F32)
        q_rest = sb("q_rest", [P, S], F32)
        probs = sb("probs", [P, 2, 4, 2, 2 * S], F32)
        eye_f = sb("eye_f", [P, P], F32)
        eye_b = sb("eye_b", [P, P], BF16)
        wq_sb = sb("wq_sb", [P, D], F32)
        wk_sb = sb("wk_sb", [P, D], F32)
        wv_sb = sb("wv_sb", [P, D], F32)
        wo_sb = sb("wo_sb", [P, D], F32)
        wg_sb = sb("wg_sb", [P, E], F32)
        w1_sb = sb("w1_sb", [P, E, HC * P], F32)
        w2_sb = sb("w2_sb", [P, E, HC, D], F32)
        b1_sb = sb("b1_sb", [P, E, HC], F32)
        b2_sb = sb("b2_sb", [E, D], F32)
        gates_sb = sb("gates_sb", [P, 2], F32)
        gate_t = sb("gate_t", [P, 2], F32)
        ln_stats = sb("ln_stats", [P, QT, 6], F32)
        ln_mv = sb("ln_mv", [P, QT, 2], F32)
        var_eps = sb("var_eps", [P, QT], F32)
        minus_half = sb("minus_half", [P, QT], F32)
        rstd1 = sb("rstd1", [P, QT], F32)
        rstd2 = sb("rstd2", [P, QT], F32)
        xn = sb("xn", [P, QT, D], F32)
        xnT = sb("xnT", [P, S], F32)
        xn2 = sb("xn2", [P, QT, D], F32)
        xn2T = sb("xn2T", [P, S], F32)
        row_max = sb("row_max", [P, QT, 2, PAIRS], F32)
        neg_max = sb("neg_max", [P, QT, 2, PAIRS], F32)
        neg_max_parts = sb("neg_max_parts", [P, QT, M_ROWS, 2 * PAIRS], BF16)
        neg_maxT = sb("neg_maxT", [M_ROWS * H, S], BF16)
        att_sb = sb("att_sb", [P, 2, S], F32)
        den = sb("den", [P, 16], F32)
        rden = sb("rden", [P, 16], F32)
        att_n = sb("att_n", [P, QT, D], F32)
        att_nT = sb("att_nT", [P, S], F32)
        h_sb = sb("h_sb", [P, 4, HC, S], F32)
        acc = sb("acc", [P, QT, D], F32)
        out_sb = sb("out_sb", [P, QT, D], F32)
        logit_top = sb("logit_top", [P, QT, 8], F32)
        logit_d = sb("logit_d", [P, QT, E], F32)
        expert_e = sb("expert_e", [P, QT, E], F32)
        expert_sum = sb("expert_sum", [P, QT], F32)
        expert_inv = sb("expert_inv", [P, QT], F32)
        expert_p = sb("expert_p", [P, QT, E], F32)
        top_p = sb("top_p", [P, QT, 8], F32)
        top_i = sb("top_i", [P, QT, 8], U32)
        top_f = sb("top_f", [P, QT, 2], F32)
        is_top = sb("is_top", [P, 2, QT, E], F32)
        chosen = sb("chosen", [P, QT, E], F32)
        expert_no = sb("expert_no", [P, QT, E], F32)
        route_w = sb("route_w", [P, QT, E], F32)
        route_wT = sb("route_wT", [E, S], F32)
        any_col = sb("any_col", [P, 1], F32)
        any_row = sb("any_row", [1, 1], F32)
        any_flag = sb("any_flag", [1, 1], I32)

        bank = [stack.enter_context(nc.psum_tensor(f"bank{i}", [P, 512], F32)) for i in range(4, 8)]
        st_bank = stack.enter_context(nc.psum_tensor("st_bank", [P, 2, 512], F32))
        mx_bank = stack.enter_context(nc.psum_tensor("mx_bank", [P, 2, 512], F32))
        av_bank, h_bank, y_bank, misc = bank

        k_scratch = nc.dram_tensor("k_scratch", [2, 3, P, S2], BF16, kind="Internal").ap()
        q_scratch = nc.dram_tensor("q_scratch", [2, 3, P, S], BF16, kind="Internal").ap()

        max_scratch = nc.dram_tensor("max_scratch", [2, M_ROWS * H, S], BF16, kind="Internal").ap()

        x_in = sem("x_in")
        x_rest_in = sem("x_rest_in")
        w_in = sem("w_in")
        mask_in = sem("mask_in")
        ffn_in = sem("ffn_in")
        batch_mask_in = [sem(f"batch_mask_in{p}") for p in range(2)]
        ctx_in = [sem(f"ctx_in{p}") for p in range(2)]
        max_scratch_out = sem("max_scratch_out")
        q_scratch_out = sem("q_scratch_out")
        k_scratch_out = sem("k_scratch_out")
        stack_in = [sem(f"stack_in{p}") for p in range(2)]
        neg_max_in = [sem(f"neg_max_in{p}") for p in range(2)]
        out_done = sem("out_done")
        stack_ones = sem("stack_ones")
        v_filled = sem("v_filled")
        numbers_set = sem("numbers_set")
        eye_b_set = sem("eye_b_set")
        half_set = sem("half_set")
        gates_set = sem("gates_set")
        any_col_set = sem("any_col_set")
        any_mm = sem("any_mm")
        any_row_set = sem("any_row_set")
        any_flag_set = sem("any_flag_set")
        ln1_step = sem("ln1_step")
        rstd1_ready = sem("rstd1_ready")
        xn_ready = sem("xn_ready")
        xnT_mm = sem("xnT_mm")
        xnT_ready = sem("xnT_ready")
        q_mm = sem("q_mm")
        k_mm = sem("k_mm")
        v_mm = sem("v_mm")
        q1_ready = sem("q1_ready")
        q_rest_ready = sem("q_rest_ready")
        q_low_ready = sem("q_low_ready")
        k1_ready = sem("k1_ready")
        k_rest_ready = sem("k_rest_ready")
        k_low_ready = sem("k_low_ready")
        v_ready = sem("v_ready")
        maskb_ready = sem("maskb_ready")
        mx_mm = sem("mx_mm")
        mx_read = sem("mx_read")
        neg_max_step = sem("neg_max_step")
        neg_max_mm = sem("neg_max_mm")
        neg_maxT_ready = sem("neg_maxT_ready")
        st_mm = sem("st_mm")
        probs_ready = sem("probs_ready")
        av_mm = sem("av_mm")
        att_ready = sem("att_ready")
        attT_mm = sem("attT_mm")
        den_step = sem("den_step")
        att_n_ready = sem("att_n_ready")
        att_nT_mm = sem("att_nT_mm")
        att_nT_ready = sem("att_nT_ready")
        proj_mm = sem("proj_mm")
        x2_ready = sem("x2_ready")
        ln2_step = sem("ln2_step")
        rstd2_ready = sem("rstd2_ready")
        xn2_ready = sem("xn2_ready")
        xn2T_mm = sem("xn2T_mm")
        xn2T_ready = sem("xn2T_ready")
        logits_mm = sem("logits_mm")
        logits_step = sem("logits_step")
        logits_read = sem("logits_read")
        expert_e_ready = sem("expert_e_ready")
        route_step = sem("route_step")
        route_ready = sem("route_ready")
        routeT_mm = sem("routeT_mm")
        routeT_ready = sem("routeT_ready")
        b2_mm = sem("b2_mm")
        acc_set = sem("acc_set")
        h_mm = sem("h_mm")
        h_ready = sem("h_ready")
        y_mm = sem("y_mm")
        acc_step = sem("acc_step")
        out_ready = sem("out_ready")

        block = stack.enter_context(nc.Block())

        @block.sync
        def _(sp):
            x_tiles = x.rearrange("b (t p) d -> p (b t) d", p=P)

            mask_tiles = mask.rearrange("b (t p) k -> p (b t) k", p=P)

            def load_batch(n):
                if not n.early:
                    hold(sp, v_mm, count(n, 1, -1))
                sp.dma_start(ctx_sb[n.par][:, :], ctxT[bass.ds(n.n, 1)].rearrange("b d k -> d (b k)")
                             ).then_inc(ctx_in[n.par], 16)
                if not n.early:
                    hold(sp, maskb_ready, count(n, 1, -1))
                sp.dma_start(mask_sb[n.par][:, :, :], mask_tiles[:, n.tiles(), :]).then_inc(batch_mask_in[n.par], 16)

            sp.dma_start(x_all[:, 0:QT, :], x_tiles[:, 0:QT, :]).then_inc(x_in, 16)
            for dst, src in ((eye_f, eye), (wq_sb, wqT), (wk_sb, wkT), (wv_sb, wvT)):
                sp.dma_start(dst[:, :], src).then_inc(w_in, 16)
            load_batch(Batch(0, 0))
            sp.dma_start(mask_all[:, :, :], mask_tiles).then_inc(mask_in, 16)
            sp.dma_start(gates_sb[:, :], gates).then_inc(ffn_in, 16)
            sp.dma_start(x_all[:, QT:, :], x_tiles[:, QT:, :]).then_inc(x_rest_in, 16)
            load_batch(Batch(0, 1))

            def stacks(a):
                jobs = ((q_parts, q_scratch, q_stack, Q_PARTS, q1_ready, q_low_ready, q_scratch_out, S),
                        (k_parts, k_scratch, k_stack, K_PARTS, k1_ready, k_low_ready, k_scratch_out, S2))
                for parts, scratch, _, _, high, low, written, _ in jobs:
                    hold(sp, high, count(a, 1, 1))
                    hold(sp, low, count(a, 2, 2))
                    if not a.early:
                        hold(sp, stack_in[a.par], 16 * STACK_DMAS * a.turn)
                    sp.dma_start(scratch[a.par].rearrange("t p n -> p t n"), parts[:, :, :]).then_inc(written, 16)
                if a.first:
                    sp.wait_ge(stack_ones, 2)
                if not a.early:
                    hold(sp, st_mm, count(a, 2 * UNITS, -2 * UNITS))
                for _, scratch, rows, order, _, _, written, width in jobs:
                    hold(sp, written, count(a, 16, 16))
                    for j in range(2):
                        for t, part in enumerate(order):
                            src = scratch[a.par, part, 64 * j:64 * j + 64, :].rearrange("(i d) n -> d i n", d=DK)
                            r0 = 64 * j + DK * t
                            sp.dma_start(rows[a.par][r0:r0 + DK, :, :], src).then_inc(stack_in[a.par], 16)

            def max_rows(a):
                hold(sp, neg_maxT_ready, count(a, 1, 1))
                if not a.early:
                    hold(sp, neg_max_in[a.par], 16 * MAX_DMAS * a.turn)
                sp.dma_start(max_scratch[a.par], neg_maxT[:, :]).then_inc(max_scratch_out, 16)
                hold(sp, max_scratch_out, count(a, 16, 16))
                rows = max_scratch[a.par].rearrange("(m j i) n -> j m i n", j=2, i=PAIRS)
                for j in range(2):
                    r0 = 64 * j + QK_ROWS
                    sp.dma_start(q_stack[a.par][r0:r0 + M_ROWS, :, :], rows[j]).then_inc(neg_max_in[a.par], 16)

            def store(c):
                hold(sp, out_ready, count(c, 1, 1))
                sp.dma_start(out[bass.ds(c.n, 1)].rearrange("b (t p) d -> p (b t) d", p=P), out_sb[:, :, :]
                             ).then_inc(out_done, 16)

            def step(a, b, c, e):
                if a:
                    stacks(a)
                if e:
                    load_batch(e)
                if a:
                    max_rows(a)
                if c:
                    store(c)

            stacks(Batch(0, 0))
            for dst, src in ((wo_sb[:, :], woT), (wg_sb[:, :], wg), (w1_sb[:, :, :], w1), (b1_sb[:, :, :], b1),
                             (w2_sb[:, :, :, :], w2), (b2_sb[:, :], b2)):
                sp.dma_start(dst, src).then_inc(ffn_in, 16)
            max_rows(Batch(0, 0))
            steps(sp, step)
            sp.wait_ge(out_done, 16 * B)

        @block.gpsimd
        def _(gp):
            gp.memset(minus_half[:, :], -0.5).then_inc(half_set, 1)
            for p in range(2):
                gp.memset(k_stack[p][:, :, :], 1.0).then_inc(stack_ones, 1)
            gp.iota(expert_no[:, :, :], pattern=[[0, QT], [1, E]], base=0, channel_multiplier=0,
                    allow_small_or_imprecise_dtypes=True).then_inc(numbers_set, 1)
            for p in range(2):
                gp.memset(v_sb[p][:, :, :, :], 0.0).then_inc(v_filled, 1)
            gp.wait_ge(v_filled, 2)
            for p in range(2):
                gp.memset(v_sb[p][:, :, :, DK:DK + 1], 1.0).then_inc(v_filled, 1)
            gp.wait_ge(w_in, 64)
            gp.tensor_copy(eye_b[:, :], eye_f[:, :]).then_inc(eye_b_set, 1)

            def low_parts(a, parts, rest, rest_ready, low_ready, written):
                gp.wait_ge(rest_ready, count(a, 1, 1))
                if not a.first:
                    hold(gp, written, count(a, 16, 0))
                gp.tensor_scalar(parts[:, 1, :], rest[:, :], 1.0, 1.0, ALU.mult, ALU.mult).then_inc(low_ready, 1)
                gp.wait_ge(low_ready, count(a, 2, 1))
                gp.tensor_tensor(parts[:, 2, :], rest[:, :], parts[:, 1, :], ALU.subtract).then_inc(low_ready, 1)

            def rstd(n, step_sem, dst, ready):
                hold(gp, step_sem, count(n, 5, 5))
                gp.tensor_tensor(dst[:, :], var_eps[:, :], minus_half[:, :], ALU.pow).then_inc(ready, 1)

            def prepare(a):
                if not a.early:
                    gp.wait_ge(st_mm, count(a, 2 * UNITS, -2 * UNITS))
                hold(gp, batch_mask_in[a.par], 16 * (a.turn + 1))
                gp.tensor_scalar(maskb[a.par][:, :, :], mask_sb[a.par][:, :, :], MASKED, 1.0, ALU.mult, ALU.mult
                                 ).then_inc(maskb_ready, 1)
                low_parts(a, q_parts, q_rest, q_rest_ready, q_low_ready, q_scratch_out)
                low_parts(a, k_parts, k_rest, k_rest_ready, k_low_ready, k_scratch_out)

            def step(a, b, c, e):
                if a:
                    prepare(a)
                if c:
                    rstd(c, ln2_step, rstd2, rstd2_ready)
                if e:
                    rstd(e, ln1_step, rstd1, rstd1_ready)

            gp.wait_ge(half_set, 1)
            rstd(Batch(0, 0), ln1_step, rstd1, rstd1_ready)
            prepare(Batch(0, 0))
            rstd(Batch(0, 1), ln1_step, rstd1, rstd1_ready)
            steps(gp, step)

        @block.tensor
        def _(pe):
            def transpose_x(a):
                pe.wait_ge(xn_ready, count(a, 1, 1))
                if a.first:
                    pe.wait_ge(w_in, 64)
                if not a.first:
                    pe.wait_ge(neg_maxT_ready, count(a, 1, 0))
                for t in range(QT):
                    mm = pe.transpose(misc[:, t * P:(t + 1) * P], xn[:, t, :], eye_f[:, :])
                mm.then_inc(xnT_mm, 1)

            def project_q(a):
                pe.wait_ge(xnT_ready, count(a, 1, 1))
                pe.matmul(misc[:, 0:S], wq_sb[:, :], xnT[:, :], start=True, stop=True).then_inc(q_mm, 1)

            def project_k(a, c):
                pe.wait_ge(ctx_in[a.par], 16 * (a.turn + 1))
                pe.wait_ge(q_rest_ready, count(a, 1, 1))
                if c:
                    pe.wait_ge(att_n_ready, count(c, 2, 2))
                pe.matmul(misc[:, :], wk_sb[:, :], ctx_sb[a.par][:, :], start=True, stop=True).then_inc(k_mm, 1)

            def project_v(a, c):
                pe.wait_ge(k_rest_ready, count(a, 1, 1))
                if c:
                    pe.wait_ge(att_nT_ready, count(c, 1, 1))
                for ch in range(KC):
                    mm = pe.matmul(misc[:, ch * P:(ch + 1) * P], ctx_sb[a.par][:, ch * P:(ch + 1) * P], wv_sb[:, :],
                                   start=True, stop=True)
                mm.then_inc(v_mm, 1)

            def max_scores(a, v, masked):
                qt, i = MX_UNITS[v]
                if v == 0:
                    pe.wait_ge(stack_in[a.par], 16 * STACK_DMAS * (a.turn + 1))
                    if masked:
                        pe.wait_ge(eye_b_set, 1)
                        pe.wait_ge(maskb_ready, count(a, 1, 1))
                if not (a.first and v == 0):
                    pe.wait_ge(mx_read, count(a, UNITS, v))
                for j in range(2):
                    r0 = 64 * j
                    mm = pe.matmul(mx_bank[:, j, :], q_stack[a.par][r0:r0 + QK_ROWS, i, qt * P:(qt + 1) * P],
                                   k_stack[a.par][r0:r0 + QK_ROWS, i, :], start=True, stop=not masked)
                if masked:
                    for j in range(2):
                        mm = pe.matmul(mx_bank[:, j, :], eye_b[:, :], maskb[a.par][:, qt, :], start=False, stop=True)
                mm.then_inc(mx_mm, 1)

            def transpose_max(a):
                pe.wait_ge(neg_max_step, count(a, 3, 3))
                pe.wait_ge(eye_b_set, 1)
                out_t = misc[:, :].bitcast(BF16)
                for t in range(QT):
                    mm = pe.transpose(out_t[0:M_ROWS * H, t * P:(t + 1) * P],
                                      neg_max_parts[:, t, :, :].rearrange("p m h -> p (m h)"), eye_b[:, :])
                mm.then_inc(neg_max_mm, 1)

            def scores(b, u, masked):
                i, half = divmod(u, 2)
                if u == 0:
                    pe.wait_ge(neg_max_in[b.par], 16 * MAX_DMAS * (b.turn + 1))
                if not (b.first and u == 0):
                    pe.wait_ge(probs_ready, count(b, 2 * UNITS, 2 * u))
                for cc in range(2):
                    for j in range(2):
                        r0, ch = 64 * j, 2 * half + cc
                        rows = QK_ROWS + M_ROWS
                        mm = pe.matmul(st_bank[:, j, cc * S:(cc + 1) * S],
                                       k_stack[b.par][r0:r0 + rows, i, ch * P:(ch + 1) * P],
                                       q_stack[b.par][r0:r0 + rows, i, :], start=True, stop=not masked)
                        if masked:
                            for t in range(QT):
                                mm = pe.matmul(st_bank[:, j, cc * S + t * P:cc * S + (t + 1) * P],
                                               maskb[b.par][:, t, ch * P:(ch + 1) * P], eye_b[:, :],
                                               start=False, stop=(t == QT - 1), skip_group_check=True)
                        if cc == 1:
                            mm.then_inc(st_mm, 1)

            def values(b, g):
                pe.wait_ge(probs_ready, count(b, 2 * UNITS, 8 * (g + 1)))
                if g == 0:
                    pe.wait_ge(v_ready, count(b, 1, 1))
                if g % 2 == 0 and not (b.first and g == 0):
                    pe.wait_ge(att_ready, count(b, 2, g // 2))
                for ch in range(KC):
                    for jj in range(4):
                        unit = 2 * (jj // 2) + ch // 2
                        cc = ch % 2
                        mm = pe.matmul(av_bank[VW * jj:VW * (jj + 1), (g % 2) * S:(g % 2 + 1) * S],
                                       v_sb[b.par][:, ch, 4 * g + jj, :],
                                       probs[:, g % 2, unit, jj % 2, cc * S:(cc + 1) * S],
                                       start=(ch == 0), stop=(ch == KC - 1), skip_group_check=True)
                mm.then_inc(av_mm, 1)

            def transpose_heads(b, hh, a):
                pe.wait_ge(att_ready, count(b, 2, hh + 1))
                if hh == 1 and a:
                    pe.wait_ge(q_rest_ready, count(a, 1, 1))
                for t in range(QT):
                    for gl in range(2):
                        k = 2 * t + gl
                        mm = pe.transpose(misc[:, k * P:(k + 1) * P], att_sb[:, gl, t * P:(t + 1) * P], eye_f[:, :])
                mm.then_inc(attT_mm, 1)

            def transpose_normed(c, a):
                pe.wait_ge(att_n_ready, count(c, 2, 2))
                if a:
                    pe.wait_ge(k_rest_ready, count(a, 1, 1))
                for t in range(QT):
                    mm = pe.transpose(misc[:, t * P:(t + 1) * P], att_n[:, t, :], eye_f[:, :])
                mm.then_inc(att_nT_mm, 1)

            def project_out(c, a):
                pe.wait_ge(att_nT_ready, count(c, 1, 1))
                if c.first:
                    pe.wait_ge(ffn_in, 16 * 7)
                if a:
                    pe.wait_ge(v_ready, count(a, 1, 1))
                for t in range(QT):
                    mm = pe.matmul(misc[:, t * P:(t + 1) * P], att_nT[:, t * P:(t + 1) * P], wo_sb[:, :],
                                   start=True, stop=True)
                mm.then_inc(proj_mm, 1)

            def transpose_x2(c):
                pe.wait_ge(xn2_ready, count(c, 1, 1))
                for t in range(QT):
                    mm = pe.transpose(misc[:, t * P:(t + 1) * P], xn2[:, t, :], eye_f[:, :])
                mm.then_inc(xn2T_mm, 1)

            def gate(c):
                pe.wait_ge(xn2T_ready, count(c, 1, 1))
                for t in range(QT):
                    mm = pe.matmul(misc[:, t * E:(t + 1) * E], xn2T[:, t * P:(t + 1) * P], wg_sb[:, :],
                                   start=True, stop=True)
                mm.then_inc(logits_mm, 1)

            def transpose_route(c):
                pe.wait_ge(route_ready, count(c, 1, 1))
                for t in range(QT):
                    mm = pe.transpose(misc[0:E, t * P:(t + 1) * P], route_w[:, t, :], eye_f[:, :])
                mm.then_inc(routeT_mm, 1)

            def bias2(c):
                pe.wait_ge(routeT_ready, count(c, 1, 1))
                for t in range(QT):
                    mm = pe.matmul(misc[:, t * P:(t + 1) * P], route_wT[:, t * P:(t + 1) * P], b2_sb[:, :],
                                   start=True, stop=True)
                mm.then_inc(b2_mm, 1)

            def hidden(c, x_):
                if not (c.first and x_ == 0):
                    pe.wait_ge(h_ready, count(c, 2 * E, 2 * x_))
                for ch in range(HC):
                    mm = pe.matmul(h_bank[:, ch * S:(ch + 1) * S], w1_sb[:, x_, ch * P:(ch + 1) * P], xn2T[:, :],
                                   start=True, stop=True)
                mm.then_inc(h_mm, 1)

            def expert_out(c, p):
                pe.wait_ge(h_ready, count(c, 2 * E, 4 * p + 4))
                if not (c.first and p == 0):
                    pe.wait_ge(acc_step, count(c, 2 * E, 4 * p))
                for el in range(2):
                    for t in range(QT):
                        k = 2 * el + t
                        for ch in range(HC):
                            mm = pe.matmul(y_bank[:, k * P:(k + 1) * P],
                                           h_sb[:, (2 * p + el) % 4, ch, t * P:(t + 1) * P],
                                           w2_sb[:, 2 * p + el, ch, :], start=(ch == 0), stop=(ch == HC - 1))
                mm.then_inc(y_mm, 1)

            def program(masked):
                def step(a, b, c, e):
                    for slot in range(UNITS):
                        if b:
                            scores(b, slot, masked)
                        if slot == 0:
                            if c:
                                values(c, 3)
                            if a:
                                transpose_x(a)
                        if slot == 1:
                            if a:
                                project_q(a)
                            if c:
                                transpose_heads(c, 1, a)
                        if slot == 2:
                            if a:
                                project_k(a, c)
                            if c:
                                transpose_normed(c, a)
                        if slot == 3:
                            if a:
                                project_v(a, c)
                            if c:
                                project_out(c, a)
                        if b and slot in (5, 9, 13):
                            values(b, (slot - 5) // 4)
                        if a:
                            for v in mx_units(slot):
                                max_scores(a, v, masked)
                        if c:
                            if slot == 6:
                                transpose_x2(c)
                            if slot == 7:
                                gate(c)
                            if EXPERT_SLOT <= slot < EXPERT_SLOT + E:
                                hidden(c, slot - EXPERT_SLOT)
                            if slot == 9:
                                transpose_route(c)
                            if slot == 10:
                                bias2(c)
                            if slot in (9, 11, 13, 15):
                                expert_out(c, (slot - 9) // 2)
                        if b and slot == 11:
                            if c:
                                pe.wait_ge(acc_set, count(c, 1, 1))
                            elif a:
                                pe.wait_ge(v_ready, count(a, 1, 1))
                            transpose_heads(b, 0, None)
                        if a and slot == 15:
                            pe.wait_ge(att_n_ready, count(b, 2, 1))
                            transpose_max(a)

                for v in range(UNITS):
                    max_scores(Batch(0, 0), v, masked)
                transpose_max(Batch(0, 0))
                steps(pe, step)

            first = Batch(0, 0)
            transpose_x(first)
            project_q(first)
            project_k(first, None)
            project_v(first, None)
            pe.wait_ge(any_col_set, 1)
            pe.wait_ge(v_ready, 1)
            pe.transpose(misc[0:1, 0:P], any_col[:, :], eye_f[:, :]).then_inc(any_mm, 1)
            pe.wait_ge(any_flag_set, 1)
            any_masked = pe.value_load(any_flag[0:1, 0:1])
            with pe.If(any_masked > 0):
                program(True)
            with pe.Else():
                program(False)

        @block.scalar
        def _(act):
            act.wait_ge(ffn_in, 16)
            act.activation(gate_t[:, :], gates_sb[:, :], ACT.Tanh).then_inc(gates_set, 1)

            def copy_xnT(a):
                act.wait_ge(xnT_mm, count(a, 1, 1))
                act.copy(xnT[:, :], misc[:, 0:S]).then_inc(xnT_ready, 1)

            def high_part(a, mm, written, parts, width, ready):
                act.wait_ge(mm, count(a, 1, 1))
                if not a.first:
                    act.wait_ge(written, count(a, 16, 0))
                act.copy(parts[:, 0, :], misc[:, 0:width]).then_inc(ready, 1)

            def copy_v(a):
                act.wait_ge(v_mm, count(a, 1, 1))
                if a.first:
                    act.wait_ge(v_filled, 4)
                if not a.early:
                    act.wait_ge(av_mm, count(a, 4, -4))
                act.copy(v_sb[a.par][:, :, :, 0:DK].rearrange("p c h d -> p (c h) d"),
                         misc[:, :].rearrange("p (c d) -> p c d", d=DK)).then_inc(v_ready, 1)

            def exps(b, u):
                g = u // 4
                for j in range(2):
                    act.wait_ge(st_mm, count(b, 2 * UNITS, 2 * u + j + 1))
                    if j == 0 and u % 4 == 0 and not (b.first and g < 2):
                        act.wait_ge(av_mm, count(b, 4, g - 1))
                    act.activation(probs[:, g % 2, u % 4, j, :], st_bank[:, j, :], ACT.Exp, scale=SCALE
                                   ).then_inc(probs_ready, 1)

            def copy_heads(b, hh):
                act.wait_ge(av_mm, count(b, 4, 2 * hh + 2))
                if not (b.first and hh == 0):
                    act.wait_ge(attT_mm, count(b, 2, hh))
                act.copy(att_sb[:, :, :].rearrange("p g s -> p (g s)"), av_bank[:, :]).then_inc(att_ready, 1)

            def copy_normed(c):
                act.wait_ge(att_nT_mm, count(c, 1, 1))
                act.copy(att_nT[:, :], misc[:, 0:S]).then_inc(att_nT_ready, 1)

            def copy_x2T(c):
                act.wait_ge(xn2T_mm, count(c, 1, 1))
                act.copy(xn2T[:, :], misc[:, 0:S]).then_inc(xn2T_ready, 1)

            def route_exp(c):
                act.wait_ge(logits_read, count(c, 1, 1))
                act.activation(expert_e[:, :, :], logit_d[:, :, :], ACT.Exp).then_inc(expert_e_ready, 1)

            def copy_routeT(c):
                act.wait_ge(routeT_mm, count(c, 1, 1))
                act.copy(route_wT[:, :], misc[0:E, 0:S]).then_inc(routeT_ready, 1)

            def set_acc(c):
                act.wait_ge(b2_mm, count(c, 1, 1))
                if not c.first:
                    act.wait_ge(out_ready, count(c, 1, 0))
                act.copy(acc[:, :, :].rearrange("p t d -> p (t d)"), misc[:, 0:S]).then_inc(acc_set, 1)

            def relu(c, x_):
                if x_ % 2 == 0 and not (c.first and x_ < 4):
                    act.wait_ge(y_mm, count(c, 4, x_ // 2 - 1))
                act.wait_ge(h_mm, count(c, E, x_ + 1))
                for ch in range(HC):
                    act.activation(h_sb[:, x_ % 4, ch, :], h_bank[:, ch * S:(ch + 1) * S], ACT.Relu,
                                   bias=b1_sb[:, x_, ch:ch + 1]).then_inc(h_ready, 1)

            def step(a, b, c, e):
                for slot in range(UNITS):
                    if b:
                        exps(b, slot)
                    if slot == 0:
                        if c:
                            copy_heads(c, 1)
                        if a:
                            copy_xnT(a)
                    if slot == 1 and a:
                        high_part(a, q_mm, q_scratch_out, q_parts, S, q1_ready)
                    if slot == 2:
                        if a:
                            high_part(a, k_mm, k_scratch_out, k_parts, S2, k1_ready)
                        if c:
                            copy_normed(c)
                    if slot == 3 and a:
                        copy_v(a)
                    if c:
                        if slot == 6:
                            copy_x2T(c)
                        if EXPERT_SLOT <= slot < EXPERT_SLOT + E:
                            relu(c, slot - EXPERT_SLOT)
                        if slot == 7:
                            route_exp(c)
                        if slot == 9:
                            copy_routeT(c)
                        if slot == 10:
                            set_acc(c)
                    if b and slot == 10:
                        copy_heads(b, 0)

            first = Batch(0, 0)
            copy_xnT(first)
            high_part(first, q_mm, q_scratch_out, q_parts, S, q1_ready)
            high_part(first, k_mm, k_scratch_out, k_parts, S2, k1_ready)
            copy_v(first)
            act.wait_ge(ffn_in, 16 * 7)
            steps(act, step)

        @block.vector
        def _(dve):
            def layernorm(n, step_sem, rstd_ready, ln_rstd, dst, dst_free, ready):
                for t in range(QT):
                    dve.bn_stats(ln_stats[:, t, :], x_all[:, bass.ds(2 * n.n + t, 1), :].rearrange("p t d -> p (t d)")
                                 ).then_inc(step_sem, 1)
                hold(dve, step_sem, count(n, 5, 2))
                for t in range(QT):
                    dve.bn_aggr(ln_mv[:, t, :], ln_stats[:, t, :]).then_inc(step_sem, 1)
                dve.wait_ge(step_sem, count(n, 5, 4))
                dve.tensor_scalar(var_eps[:, :], ln_mv[:, :, 1], EPS, None, ALU.add).then_inc(step_sem, 1)
                dve.wait_ge(rstd_ready, count(n, 1, 1))
                if not n.first:
                    dve.wait_ge(dst_free, count(n, 1, 0))
                for t in range(QT):
                    ln = dve.tensor_scalar(dst[:, t, :], x_all[:, bass.ds(2 * n.n + t, 1), :].rearrange("p t d -> p (t d)"),
                                           ln_mv[:, t, 0:1], ln_rstd[:, t:t + 1], ALU.subtract, ALU.mult)
                ln.then_inc(ready, 1)

            def rest(a, high, parts, dst, width, low, ready):
                dve.wait_ge(high, count(a, 1, 1))
                if not a.first:
                    dve.wait_ge(low, count(a, 2, 0))
                dve.tensor_tensor(dst[:, :], misc[:, 0:width], parts[:, 0, :], ALU.subtract).then_inc(ready, 1)

            def reduce_max(a, v):
                qt, i = MX_UNITS[v]
                dve.wait_ge(mx_mm, count(a, UNITS, v + 1))
                dve.tensor_reduce(row_max[:, qt, :, i], mx_bank[:, :, :], AX_X, ALU.max).then_inc(mx_read, 1)

            def negate_max(a):
                dve.wait_ge(mx_read, count(a, UNITS, UNITS))
                dve.tensor_scalar(neg_max[:, :, :, :], row_max[:, :, :, :], LOWEST, -1.0, ALU.max, ALU.mult
                                  ).then_inc(neg_max_step, 1)
                dve.wait_ge(neg_max_step, count(a, 3, 1))
                if not a.first:
                    dve.wait_ge(neg_max_mm, count(a, 1, 0))
                src = neg_max[:, :, :, :].rearrange("p t j i -> p t (j i)")
                dve.tensor_copy(neg_max_parts[:, :, 0, :], src).then_inc(neg_max_step, 1)
                dve.wait_ge(neg_max_step, count(a, 3, 2))
                dve.tensor_tensor(neg_max_parts[:, :, 1, :], src, neg_max_parts[:, :, 0, :], ALU.subtract
                                  ).then_inc(neg_max_step, 1)

            def copy_maxT(a):
                dve.wait_ge(neg_max_mm, count(a, 1, 1))
                if not a.first:
                    dve.wait_ge(max_scratch_out, count(a, 16, 0))
                dve.tensor_copy(neg_maxT[:, :], misc[:, :].bitcast(BF16)[0:M_ROWS * H, 0:S]).then_inc(neg_maxT_ready, 1)

            def normalise(b, hh):
                dve.wait_ge(attT_mm, count(b, 2, hh + 1))
                heads = misc[:, :].rearrange("p (k w) -> p k w", w=VW)
                dve.tensor_scalar(den[:, :], heads[:, :, DK], 1e-30, None, ALU.max).then_inc(den_step, 1)
                dve.wait_ge(den_step, count(b, 4, 2 * hh + 1))
                dve.reciprocal(rden[:, :], den[:, :]).then_inc(den_step, 1)
                dve.wait_ge(den_step, count(b, 4, 2 * hh + 2))
                if hh == 0 and not b.first:
                    dve.wait_ge(att_nT_mm, count(b, 1, 0))
                half = H // 2
                dve.tensor_tensor(
                    att_n[:, :, hh * 64:(hh + 1) * 64].rearrange("p t (h d) -> p t h d", d=DK),
                    misc[:, :].rearrange("p (t h w) -> p t h w", t=QT, h=half)[:, :, :, 0:DK],
                    rden[:, :].rearrange("p (t h) -> p t h", t=QT).unsqueeze(3).to_broadcast([P, QT, half, DK]),
                    ALU.mult).then_inc(att_n_ready, 1)

            def residual(c):
                dve.wait_ge(proj_mm, count(c, 1, 1))
                if c.first:
                    dve.wait_ge(gates_set, 1)
                xt = x_all[:, c.tiles(), :]
                dve.scalar_tensor_tensor(out=xt, in0=misc[:, 0:S].rearrange("p (t d) -> p t d", t=QT),
                                         scalar=gate_t[:, 0:1], in1=xt, op0=ALU.mult, op1=ALU.add).then_inc(x2_ready, 1)
                hold(dve, x2_ready, count(c, 1, 1))

            def logits(c):
                hold(dve, logits_mm, count(c, 1, 1))
                lg = misc[:, 0:QT * E].rearrange("p (t e) -> p t e", t=QT)
                for t in range(QT):
                    dve.max(logit_top[:, t, :], lg[:, t, :]).then_inc(logits_step, 1)
                dve.wait_ge(logits_step, count(c, 2, 2))
                dve.tensor_tensor(logit_d[:, :, :], lg, logit_top[:, :, 0:1].to_broadcast([P, QT, E]), ALU.subtract
                                  ).then_inc(logits_read, 1)

            def route(c):
                k = [0]

                def link(ins, need=True):
                    k[0] += 1
                    ins.then_inc(route_step, 1)
                    if need:
                        hold(dve, route_step, count(c, ROUTE_STEPS, k[0]))

                dve.wait_ge(expert_e_ready, count(c, 1, 1))
                link(dve.tensor_reduce(expert_sum[:, :], expert_e[:, :, :], AX_X, ALU.add))
                link(dve.reciprocal(expert_inv[:, :], expert_sum[:, :]))
                link(dve.tensor_tensor(expert_p[:, :, :], expert_e[:, :, :],
                                       expert_inv[:, :].unsqueeze(2).to_broadcast([P, QT, E]), ALU.mult))
                for t in range(QT):
                    top = dve.max(top_p[:, t, :], expert_p[:, t, :])
                link(top)
                for t in range(QT):
                    top = dve.max_index(top_i[:, t, :], top_p[:, t, :], expert_p[:, t, :])
                link(top)
                link(dve.tensor_copy(top_f[:, :, :], top_i[:, :, 0:2]))
                for m in range(2):
                    link(dve.tensor_tensor(is_top[:, m, :, :], expert_no[:, :, :],
                                           top_f[:, :, m:m + 1].to_broadcast([P, QT, E]), ALU.is_equal), m == 1)
                link(dve.tensor_tensor(chosen[:, :, :], is_top[:, 0, :, :], is_top[:, 1, :, :], ALU.add))
                if not c.first:
                    dve.wait_ge(routeT_mm, count(c, 1, 0))
                assert k[0] == ROUTE_STEPS
                dve.tensor_tensor(route_w[:, :, :], chosen[:, :, :], expert_p[:, :, :], ALU.mult
                                  ).then_inc(route_ready, 1)

            def add_experts(c, p):
                dve.wait_ge(y_mm, count(c, 4, p + 1))
                for el in range(2):
                    x_ = 2 * p + el
                    if x_ == 0:
                        dve.wait_ge(acc_set, count(c, 1, 1))
                        dve.wait_ge(route_ready, count(c, 1, 1))
                    else:
                        dve.wait_ge(acc_step, count(c, 2 * E, 2 * x_))
                    for t in range(QT):
                        k = 2 * el + t
                        dve.scalar_tensor_tensor(out=acc[:, t, :], in0=y_bank[:, k * P:(k + 1) * P],
                                                 scalar=route_w[:, t, x_:x_ + 1], in1=acc[:, t, :],
                                                 op0=ALU.mult, op1=ALU.add).then_inc(acc_step, 1)

            def finish(c):
                dve.wait_ge(acc_step, count(c, 2 * E, 2 * E))
                if not c.first:
                    dve.wait_ge(out_done, count(c, 16, 0))
                dve.scalar_tensor_tensor(out=out_sb[:, :, :], in0=acc[:, :, :], scalar=gate_t[:, 1:2],
                                         in1=x_all[:, c.tiles(), :], op0=ALU.mult, op1=ALU.add).then_inc(out_ready, 1)

            def step(a, b, c, e):
                for slot in range(UNITS):
                    if slot == 1:
                        if a:
                            rest(a, q1_ready, q_parts, q_rest, S, q_low_ready, q_rest_ready)
                        if c:
                            normalise(c, 1)
                    if slot == 2 and a:
                        rest(a, k1_ready, k_parts, k_rest, S2, k_low_ready, k_rest_ready)
                    if slot == 3 and c:
                        residual(c)
                        layernorm(c, ln2_step, rstd2_ready, rstd2, xn2, xn2T_mm, xn2_ready)
                    if a:
                        for v in mx_units(slot):
                            reduce_max(a, v)
                    if c:
                        if slot == 7:
                            logits(c)
                        if slot == 8:
                            route(c)
                        if slot in (9, 11, 13, 15):
                            if slot > 9:
                                add_experts(c, (slot - 11) // 2)
                    if b and slot == 12:
                        normalise(b, 0)
                    if e and slot == 13:
                        layernorm(e, ln1_step, rstd1_ready, rstd1, xn, xnT_mm, xn_ready)
                    if a and slot == 14:
                        negate_max(a)
                    if a and slot == 15:
                        copy_maxT(a)
                    if c and slot == 15:
                        add_experts(c, 3)
                        finish(c)

            first = Batch(0, 0)
            dve.wait_ge(x_in, 16)
            layernorm(first, ln1_step, rstd1_ready, rstd1, xn, None, xn_ready)
            rest(first, q1_ready, q_parts, q_rest, S, q_low_ready, q_rest_ready)
            rest(first, k1_ready, k_parts, k_rest, S2, k_low_ready, k_rest_ready)
            dve.wait_ge(mask_in, 16)
            dve.tensor_reduce(any_col[:, :], mask_all[:, :, :].rearrange("p t k -> p (t k)").bitcast(I32), AX_X, ALU.max
                              ).then_inc(any_col_set, 1)
            dve.wait_ge(any_mm, 1)
            dve.tensor_reduce(any_row[:, :], misc[0:1, 0:P], AX_X, ALU.max).then_inc(any_row_set, 1)
            dve.wait_ge(any_row_set, 1)
            dve.tensor_scalar(any_flag[:, :], any_row[:, :], 1.0, None, ALU.min).then_inc(any_flag_set, 1)
            dve.wait_ge(x_rest_in, 16)
            layernorm(Batch(0, 1), ln1_step, rstd1_ready, rstd1, xn, xnT_mm, xn_ready)
            dve.wait_ge(numbers_set, 1)
            for v in range(UNITS):
                reduce_max(first, v)
            negate_max(first)
            copy_maxT(first)
            steps(dve, step)


def kernel(x, ctx_1024, mask_BxSxS2_bf0, g_xattn, g_ffn, L0_xattn_W_Q, L0_xattn_W_K, L0_xattn_W_V, L0_xattn_W_O,
           L0_ffn_Wg, L0_ffn_W1, L0_ffn_b1, L0_ffn_W2, L0_ffn_b2):
    import numpy as np
    import concourse.bacc as bacc
    from concourse.bass_utils import run_bass_kernel_spmd

    def pair_order(w):
        return np.ascontiguousarray(np.asarray(w).T.reshape(D, PAIRS, 2, DK).transpose(0, 2, 1, 3).reshape(D, D))

    arrays = {
        "x": np.asarray(x),
        "ctxT": np.ascontiguousarray(np.asarray(ctx_1024).transpose(0, 2, 1)),
        "mask": np.asarray(mask_BxSxS2_bf0),
        "gates": np.ascontiguousarray(np.broadcast_to(
            np.concatenate([np.asarray(g_xattn), np.asarray(g_ffn)])[None, :], (P, 2))),
        "wqT": pair_order(L0_xattn_W_Q),
        "wkT": pair_order(L0_xattn_W_K),
        "wvT": np.ascontiguousarray(np.asarray(L0_xattn_W_V).T),
        "woT": np.ascontiguousarray(np.asarray(L0_xattn_W_O).T),
        "wg": np.asarray(L0_ffn_Wg),
        "w1": np.ascontiguousarray(np.asarray(L0_ffn_W1).transpose(1, 0, 2)),
        "b1": np.ascontiguousarray(np.asarray(L0_ffn_b1).reshape(E, HC, P).transpose(2, 0, 1)),
        "w2": np.ascontiguousarray(np.asarray(L0_ffn_W2).reshape(E, HC, P, D).transpose(2, 0, 1, 3)),
        "b2": np.asarray(L0_ffn_b2),
        "eye": np.eye(P, dtype=np.float32),
    }
    nc = bacc.Bacc("TRN2", target_bir_lowering=False, num_devices=1)
    args = {name: nc.dram_tensor(f"in_{name}", a.shape, mybir.dt.from_np(a.dtype), kind="ExternalInput").ap()
            for name, a in arrays.items()}
    result = nc.dram_tensor("out_0", (B, S, D), F32, kind="ExternalOutput").ap()
    build(nc, out=result, **args)
    run = run_bass_kernel_spmd(nc, [{f"in_{name}": a for name, a in arrays.items()}], core_ids=[0])
    return run.results[0]["out_0"]
```

```python
from contextlib import ExitStack

import concourse.bass as bass
from concourse import mybir

F32 = mybir.dt.float32
BF16 = mybir.dt.bfloat16
U8 = mybir.dt.uint8
U32 = mybir.dt.uint32
I32 = mybir.dt.int32
ALU = mybir.AluOpType
ACT = mybir.ActivationFunctionType
AX_X = mybir.AxisListType.X

P = 128
B = 8
S = 256
S2 = 512
D = 128
H = 16
DK = D // H
QT = S // P
KC = S2 // P
PAIRS = H // 2
E = 8
HC = 2
VW = 32
UNITS = 2 * PAIRS
GROUPS = 4
SCALE = 1.0 / float(DK) ** 0.5
EPS = 1e-5
MASKED = -1e30
LOWEST = -1e29

K_PARTS = [0, 0, 0, 1, 1, 2]
Q_PARTS = [0, 1, 2, 0, 1, 0]
TERMS = len(K_PARTS)
QK_ROWS = TERMS * DK
M_ROWS = 2
STACK_DMAS = 2 * (TERMS + TERMS)
MAX_DMAS = 2
HALF = PAIRS // 2

MX_UNITS = [(i, qt) for i in range(PAIRS) for qt in range(QT)]
HIDDEN_SLOTS = {9: 0, 11: 1, 13: 2, 15: 3, 1: 4, 3: 5, 5: 6, 7: 7}
OUT_SLOTS = {13: 0, 1: 1, 5: 2, 8: 3}
ADD_SLOTS = {14: 0, 2: 1, 6: 2, 9: 3}
OUT_NEXT = 10
ROUTE_STEPS = 9


class Batch:

    def __init__(self, r, off):
        self.n = 2 * r + off
        self.turn = r + off // 2
        self.par = off % 2
        self.first = isinstance(self.n, int) and self.n == 0
        self.early = isinstance(self.n, int) and self.n < 2

    def tiles(self):
        return bass.ds(2 * self.n, QT)


def count(batch, per, k):
    return per * batch.n + k


def hold(engine, semaphore, value):
    engine.wait_ge(semaphore, value)
    engine.nop(nofuse=True)


def first_step(step):
    step(Batch(0, 0), None, None, None, None)


def later_steps(engine, step):
    def at(r, off):
        return tuple(Batch(r, off + k) if not isinstance(r, int) or 0 <= off + k < B else None for k in (2, 1, 0, -1, -2))

    for s in (-1, 0, 1):
        step(*at(0, s))
    with engine.Fori(0, 2) as r:
        step(*at(r, 2))
        step(*at(r, 3))
    for s in (6, 7, 8, 9):
        step(*at(0, s))


def build(nc, x, ctxT, mask, gates, wqT, wkT, wvT, woT, wg, w1, b1, w2, b2, eye, out):
    with ExitStack() as stack:
        def sb(name, shape, dt):
            return stack.enter_context(nc.sbuf_tensor(name, shape, dt))

        def sem(name):
            return stack.enter_context(nc.semaphore(name))

        x_all = sb("x_all", [P, B * QT, D], F32)
        mask_all = sb("mask_all", [P, B * QT, S2], U8)
        mask_sb = [sb(f"mask_sb{p}", [P, QT, S2], U8) for p in range(2)]
        ctx_sb = [sb(f"ctx_sb{p}", [P, S2], F32) for p in range(2)]
        maskb = [sb(f"maskb{p}", [P, QT, S2], BF16) for p in range(2)]
        k_stack = [sb(f"k_stack{p}", [P, PAIRS, S2], BF16) for p in range(2)]
        q_stack = [sb(f"q_stack{p}", [P, PAIRS, S], BF16) for p in range(2)]
        v_sb = [sb(f"v_sb{p}", [P, KC, H, VW], F32) for p in range(2)]
        k_parts = sb("k_parts", [P, 3, S2], BF16)
        q_parts = sb("q_parts", [P, 3, S], BF16)
        k_rest = sb("k_rest", [P, S2], F32)
        q_rest = sb("q_rest", [P, S], F32)
        probs = sb("probs", [P, 2, 4, 2, 2 * S], F32)
        eye_f = sb("eye_f", [P, P], F32)
        eye_b = sb("eye_b", [P, P], BF16)
        wq_sb = sb("wq_sb", [P, D], F32)
        wk_sb = sb("wk_sb", [P, D], F32)
        wv_sb = sb("wv_sb", [P, D], F32)
        wo_sb = sb("wo_sb", [P, D], F32)
        wg_sb = sb("wg_sb", [P, E], F32)
        w1_sb = sb("w1_sb", [P, E, HC * P], F32)
        w2_sb = sb("w2_sb", [P, E, HC, D], F32)
        b1_sb = sb("b1_sb", [P, E, HC], F32)
        b2_sb = sb("b2_sb", [E, D], F32)
        gates_sb = sb("gates_sb", [P, 2], F32)
        gate_t = sb("gate_t", [P, 2], F32)
        ln_stats = sb("ln_stats", [P, QT, 6], F32)
        ln_mv = sb("ln_mv", [P, QT, 2], F32)
        var_eps = sb("var_eps", [P, QT], F32)
        minus_half = sb("minus_half", [P, QT], F32)
        rstd1 = sb("rstd1", [P, QT], F32)
        rstd2 = sb("rstd2", [P, QT], F32)
        xn = sb("xn", [P, QT, D], F32)
        xnT = sb("xnT", [P, S], F32)
        xn2 = sb("xn2", [P, QT, D], F32)
        xn2T = [sb(f"xn2T{p}", [P, S], F32) for p in range(2)]
        row_max = sb("row_max", [P, QT, 2, PAIRS], F32)
        neg_max = sb("neg_max", [P, QT, 2, HALF], F32)
        neg_max_parts = sb("neg_max_parts", [P, QT, M_ROWS, 2 * HALF], BF16)
        neg_maxT = sb("neg_maxT", [M_ROWS * 2 * HALF, S], BF16)
        att_sb = sb("att_sb", [P, 2, S], F32)
        den = sb("den", [P, 16], F32)
        rden = sb("rden", [P, 16], F32)
        att_n = sb("att_n", [P, QT, D], F32)
        att_nT = sb("att_nT", [P, S], F32)
        h_sb = sb("h_sb", [P, 4, HC, S], F32)
        acc = sb("acc", [P, QT, D], F32)
        logit_top = sb("logit_top", [P, QT, 8], F32)
        logit_d = sb("logit_d", [P, QT, E], F32)
        expert_e = sb("expert_e", [P, QT, E], F32)
        expert_sum = sb("expert_sum", [P, QT], F32)
        expert_inv = sb("expert_inv", [P, QT], F32)
        expert_p = sb("expert_p", [P, QT, E], F32)
        top_p = sb("top_p", [P, QT, 8], F32)
        top_i = sb("top_i", [P, QT, 8], U32)
        top_f = sb("top_f", [P, QT, 2], F32)
        is_top = sb("is_top", [P, 2, QT, E], F32)
        chosen = sb("chosen", [P, QT, E], F32)
        expert_no = sb("expert_no", [P, QT, E], F32)
        route_w = sb("route_w", [P, QT, E], F32)
        route_wT = sb("route_wT", [E, S], F32)
        any_col = sb("any_col", [P, 1], F32)
        any_row = sb("any_row", [1, 1], F32)
        any_flag = sb("any_flag", [1, 1], I32)

        bank = [stack.enter_context(nc.psum_tensor(f"bank{i}", [P, 512], F32)) for i in range(4, 8)]
        st_bank = stack.enter_context(nc.psum_tensor("st_bank", [P, 2, 512], F32))
        mx_bank = stack.enter_context(nc.psum_tensor("mx_bank", [P, 2, 512], F32))
        av_bank, h_bank, y_bank, misc = bank

        k_scratch = nc.dram_tensor("k_scratch", [2, 3, P, S2], BF16, kind="Internal").ap()
        q_scratch = nc.dram_tensor("q_scratch", [2, 3, P, S], BF16, kind="Internal").ap()

        max_scratch = nc.dram_tensor("max_scratch", [2, 2, M_ROWS * 2 * HALF, S], BF16, kind="Internal").ap()

        x_in = sem("x_in")
        x_rest_in = sem("x_rest_in")
        w_in = sem("w_in")
        mask_in = sem("mask_in")
        ffn_in = sem("ffn_in")
        batch_mask_in = [sem(f"batch_mask_in{p}") for p in range(2)]
        ctx_in = [sem(f"ctx_in{p}") for p in range(2)]
        max_scratch_out = sem("max_scratch_out")
        q_scratch_out = sem("q_scratch_out")
        k_scratch_out = sem("k_scratch_out")
        stack_in = [[sem(f"stack_in{p}_{half}") for half in range(2)] for p in range(2)]
        neg_max_in = [[sem(f"neg_max_in{p}_{half}") for half in range(2)] for p in range(2)]
        out_done = sem("out_done")
        stack_ones = sem("stack_ones")
        v_filled = sem("v_filled")
        numbers_set = sem("numbers_set")
        eye_b_set = sem("eye_b_set")
        half_set = sem("half_set")
        gates_set = sem("gates_set")
        any_col_set = sem("any_col_set")
        any_mm = sem("any_mm")
        any_row_set = sem("any_row_set")
        any_flag_set = sem("any_flag_set")
        ln1_step = sem("ln1_step")
        rstd1_ready = sem("rstd1_ready")
        xn_ready = sem("xn_ready")
        xnT_mm = sem("xnT_mm")
        xnT_ready = sem("xnT_ready")
        q_mm = sem("q_mm")
        k_mm = sem("k_mm")
        v_mm = sem("v_mm")
        q1_ready = sem("q1_ready")
        q_rest_ready = sem("q_rest_ready")
        q_low_ready = sem("q_low_ready")
        k1_ready = sem("k1_ready")
        k_rest_ready = sem("k_rest_ready")
        k_low_ready = sem("k_low_ready")
        v_ready = sem("v_ready")
        maskb_ready = sem("maskb_ready")
        mx_mm = sem("mx_mm")
        mx_read = sem("mx_read")
        neg_max_step = sem("neg_max_step")
        neg_max_mm = sem("neg_max_mm")
        neg_maxT_ready = sem("neg_maxT_ready")
        st_mm = sem("st_mm")
        probs_ready = sem("probs_ready")
        av_mm = sem("av_mm")
        att_ready = sem("att_ready")
        attT_mm = sem("attT_mm")
        den_step = sem("den_step")
        att_n_ready = sem("att_n_ready")
        att_nT_mm = sem("att_nT_mm")
        att_nT_ready = sem("att_nT_ready")
        proj_mm = sem("proj_mm")
        x2_ready = sem("x2_ready")
        ln2_step = sem("ln2_step")
        rstd2_ready = sem("rstd2_ready")
        xn2_ready = sem("xn2_ready")
        xn2T_mm = sem("xn2T_mm")
        xn2T_ready = sem("xn2T_ready")
        logits_mm = sem("logits_mm")
        logits_step = sem("logits_step")
        logits_read = sem("logits_read")
        expert_e_ready = sem("expert_e_ready")
        route_step = sem("route_step")
        route_ready = sem("route_ready")
        routeT_mm = sem("routeT_mm")
        routeT_ready = sem("routeT_ready")
        b2_mm = sem("b2_mm")
        acc_set = sem("acc_set")
        h_mm = sem("h_mm")
        h_ready = sem("h_ready")
        y_mm = sem("y_mm")
        acc_step = sem("acc_step")
        out_ready = sem("out_ready")

        block = stack.enter_context(nc.Block())

        @block.sync
        def _(sp):
            x_tiles = x.rearrange("b (t p) d -> p (b t) d", p=P)

            mask_tiles = mask.rearrange("b (t p) k -> p (b t) k", p=P)

            def load_ctx(n):
                if not n.early:
                    hold(sp, v_mm, count(n, 1, -1))
                sp.dma_start(ctx_sb[n.par][:, :], ctxT[bass.ds(n.n, 1)].rearrange("b d k -> d (b k)")
                             ).then_inc(ctx_in[n.par], 16)

            def load_mask(n):
                if not n.early:
                    hold(sp, maskb_ready, count(n, 1, -1))
                sp.dma_start(mask_sb[n.par][:, :, :], mask_tiles[:, n.tiles(), :]).then_inc(batch_mask_in[n.par], 16)

            sp.dma_start(x_all[:, 0:QT, :], x_tiles[:, 0:QT, :]).then_inc(x_in, 16)
            for dst, src in ((eye_f, eye), (wq_sb, wqT), (wk_sb, wkT), (wv_sb, wvT)):
                sp.dma_start(dst[:, :], src).then_inc(w_in, 16)
            sp.dma_start(mask_all[:, :, :], mask_tiles).then_inc(mask_in, 16)
            sp.dma_start(gates_sb[:, :], gates).then_inc(ffn_in, 16)
            sp.dma_start(x_all[:, QT:, :], x_tiles[:, QT:, :]).then_inc(x_rest_in, 16)

            jobs = ((q_parts, q_scratch, q_stack, Q_PARTS, q1_ready, q_low_ready, q_scratch_out),
                    (k_parts, k_scratch, k_stack, K_PARTS, k1_ready, k_low_ready, k_scratch_out))

            def write_scratch(p):
                for parts, scratch, _, _, high, low, written in jobs:
                    hold(sp, high, count(p, 1, 1))
                    hold(sp, low, count(p, 2, 2))
                    if not p.early:
                        hold(sp, stack_in[p.par][1], 16 * STACK_DMAS * p.turn)
                    sp.dma_start(scratch[p.par].rearrange("t p n -> p t n"), parts[:, :, :]).then_inc(written, 16)

            def read_stacks(p, half):
                if p.early:
                    sp.wait_ge(stack_ones, 2)
                else:
                    hold(sp, st_mm, count(p, 2 * UNITS, -4 * UNITS + UNITS * (half + 1)))
                for _, scratch, rows, order, _, _, written in jobs:
                    hold(sp, written, count(p, 16, 16))
                    pairs = slice(half * HALF, (half + 1) * HALF)
                    for j in range(2):
                        for t, part in enumerate(order):
                            c0 = 64 * j + DK * HALF * half
                            src = scratch[p.par, part, c0:c0 + DK * HALF, :].rearrange("(i d) n -> d i n", d=DK)
                            r0 = 64 * j + DK * t
                            sp.dma_start(rows[p.par][r0:r0 + DK, pairs, :], src).then_inc(stack_in[p.par][half], 16)

            def max_rows(a, half):
                hold(sp, neg_maxT_ready, count(a, 2, half + 1))
                if not a.early:
                    hold(sp, neg_max_in[a.par][half], 16 * MAX_DMAS * a.turn)
                sp.dma_start(max_scratch[a.par, half], neg_maxT[:, :]).then_inc(max_scratch_out, 16)
                hold(sp, max_scratch_out, count(a, 32, 16 * (half + 1)))
                rows = max_scratch[a.par, half].rearrange("(m j i) n -> j m i n", j=2, i=HALF)
                for j in range(2):
                    r0 = 64 * j + QK_ROWS
                    sp.dma_start(q_stack[a.par][r0:r0 + M_ROWS, half * HALF:(half + 1) * HALF, :], rows[j]
                                 ).then_inc(neg_max_in[a.par][half], 16)

            def store(d):
                hold(sp, out_ready, count(d, 1, 1))
                sp.dma_start(out[bass.ds(d.n, 1)].rearrange("b (t p) d -> p (b t) d", p=P), x_all[:, d.tiles(), :]
                             ).then_inc(out_done, 16)

            def step(p, a, b, c, d):
                if p:
                    load_ctx(p)
                if b:
                    max_rows(b, 1)
                if a:
                    read_stacks(a, 1)
                if p:
                    load_mask(p)
                    write_scratch(p)
                if d:
                    store(d)
                if p:
                    read_stacks(p, 0)
                if a:
                    max_rows(a, 0)

            first_step(step)
            for dst, src in ((wo_sb[:, :], woT), (wg_sb[:, :], wg), (w1_sb[:, :, :], w1), (b1_sb[:, :, :], b1),
                             (w2_sb[:, :, :, :], w2), (b2_sb[:, :], b2)):
                sp.dma_start(dst, src).then_inc(ffn_in, 16)
            later_steps(sp, step)
            sp.wait_ge(out_done, 16 * B)

        @block.gpsimd
        def _(gp):
            gp.memset(minus_half[:, :], -0.5).then_inc(half_set, 1)
            for p in range(2):
                gp.memset(k_stack[p][:, :, :], 1.0).then_inc(stack_ones, 1)
            gp.iota(expert_no[:, :, :], pattern=[[0, QT], [1, E]], base=0, channel_multiplier=0,
                    allow_small_or_imprecise_dtypes=True).then_inc(numbers_set, 1)
            for p in range(2):
                gp.memset(v_sb[p][:, :, :, :], 0.0).then_inc(v_filled, 1)
            gp.wait_ge(v_filled, 2)
            for p in range(2):
                gp.memset(v_sb[p][:, :, :, DK:DK + 1], 1.0).then_inc(v_filled, 1)
            gp.wait_ge(w_in, 64)
            gp.tensor_copy(eye_b[:, :], eye_f[:, :]).then_inc(eye_b_set, 1)

            def low_parts(a, parts, rest, rest_ready, low_ready, written):
                gp.wait_ge(rest_ready, count(a, 1, 1))
                if not a.first:
                    hold(gp, written, count(a, 16, 0))
                gp.tensor_scalar(parts[:, 1, :], rest[:, :], 1.0, 1.0, ALU.mult, ALU.mult).then_inc(low_ready, 1)
                gp.wait_ge(low_ready, count(a, 2, 1))
                gp.tensor_tensor(parts[:, 2, :], rest[:, :], parts[:, 1, :], ALU.subtract).then_inc(low_ready, 1)

            def rstd(n, step_sem, dst, ready):
                hold(gp, step_sem, count(n, 5, 5))
                gp.tensor_tensor(dst[:, :], var_eps[:, :], minus_half[:, :], ALU.pow).then_inc(ready, 1)

            def mask_bias(a):
                if not a.early:
                    gp.wait_ge(st_mm, count(a, 2 * UNITS, -2 * UNITS))
                hold(gp, batch_mask_in[a.par], 16 * (a.turn + 1))
                gp.tensor_scalar(maskb[a.par][:, :, :], mask_sb[a.par][:, :, :], MASKED, 1.0, ALU.mult, ALU.mult
                                 ).then_inc(maskb_ready, 1)

            def step(p, a, b, c, d):
                if p:
                    rstd(p, ln1_step, rstd1, rstd1_ready)
                if a:
                    mask_bias(a)
                if p:
                    low_parts(p, q_parts, q_rest, q_rest_ready, q_low_ready, q_scratch_out)
                if c:
                    rstd(c, ln2_step, rstd2, rstd2_ready)
                if p:
                    low_parts(p, k_parts, k_rest, k_rest_ready, k_low_ready, k_scratch_out)

            gp.wait_ge(half_set, 1)
            first_step(step)
            later_steps(gp, step)

        @block.tensor
        def _(pe):
            def transpose_x(p, a, b, c):
                pe.wait_ge(xn_ready, count(p, 1, 1))
                if p.first:
                    pe.wait_ge(w_in, 64)
                elif c:
                    pe.wait_ge(att_n_ready, count(c, 2, 2))
                elif b:
                    pe.wait_ge(neg_maxT_ready, count(b, 2, 2))
                for t in range(QT):
                    mm = pe.transpose(misc[:, t * P:(t + 1) * P], xn[:, t, :], eye_f[:, :])
                mm.then_inc(xnT_mm, 1)

            def project_q(p, c):
                pe.wait_ge(xnT_ready, count(p, 1, 1))
                if c:
                    pe.wait_ge(att_nT_ready, count(c, 1, 1))
                pe.matmul(misc[:, 0:S], wq_sb[:, :], xnT[:, :], start=True, stop=True).then_inc(q_mm, 1)

            def project_k(p, c):
                pe.wait_ge(ctx_in[p.par], 16 * (p.turn + 1))
                pe.wait_ge(q_rest_ready, count(p, 1, 1))
                if c:
                    pe.wait_ge(x2_ready, count(c, 1, 1))
                pe.matmul(misc[:, :], wk_sb[:, :], ctx_sb[p.par][:, :], start=True, stop=True).then_inc(k_mm, 1)

            def project_v(a, p, c):
                if c:
                    pe.wait_ge(logits_read, count(c, 1, 1))
                elif p:
                    pe.wait_ge(k_rest_ready, count(p, 1, 1))
                for ch in range(KC):
                    mm = pe.matmul(misc[:, ch * P:(ch + 1) * P], ctx_sb[a.par][:, ch * P:(ch + 1) * P], wv_sb[:, :],
                                   start=True, stop=True)
                mm.then_inc(v_mm, 1)

            def max_scores(a, v, masked):
                i, qt = MX_UNITS[v]
                if v % (UNITS // 2) == 0:
                    pe.wait_ge(stack_in[a.par][v // (UNITS // 2)], 16 * STACK_DMAS * (a.turn + 1))
                if v == 0:
                    if masked:
                        pe.wait_ge(eye_b_set, 1)
                        pe.wait_ge(maskb_ready, count(a, 1, 1))
                if not (a.first and v == 0):
                    pe.wait_ge(mx_read, count(a, UNITS, v))
                for j in range(2):
                    r0 = 64 * j
                    mm = pe.matmul(mx_bank[:, j, :], q_stack[a.par][r0:r0 + QK_ROWS, i, qt * P:(qt + 1) * P],
                                   k_stack[a.par][r0:r0 + QK_ROWS, i, :], start=True, stop=not masked)
                if masked:
                    for j in range(2):
                        mm = pe.matmul(mx_bank[:, j, :], eye_b[:, :], maskb[a.par][:, qt, :], start=False, stop=True)
                mm.then_inc(mx_mm, 1)

            def transpose_max(n, half, c):
                pe.wait_ge(neg_max_step, count(n, 6, 3 * (half + 1)))
                if half == 0:
                    pe.wait_ge(eye_b_set, 1)
                    pe.wait_ge(v_ready, count(n, 1, 1))
                elif c:
                    pe.wait_ge(att_n_ready, count(c, 2, 1))
                out_t = misc[:, :].bitcast(BF16)
                for t in range(QT):
                    mm = pe.transpose(out_t[0:M_ROWS * 2 * HALF, t * P:(t + 1) * P],
                                      neg_max_parts[:, t, :, :].rearrange("p m h -> p (m h)"), eye_b[:, :])
                mm.then_inc(neg_max_mm, 1)

            def scores(b, u, masked):
                i, half = divmod(u, 2)
                if u % (UNITS // 2) == 0:
                    pe.wait_ge(neg_max_in[b.par][u // (UNITS // 2)], 16 * MAX_DMAS * (b.turn + 1))
                if not (b.first and u == 0):
                    pe.wait_ge(probs_ready, count(b, 2 * UNITS, 2 * u))
                for cc in range(2):
                    for j in range(2):
                        r0, ch = 64 * j, 2 * half + cc
                        rows = QK_ROWS + M_ROWS
                        mm = pe.matmul(st_bank[:, j, cc * S:(cc + 1) * S],
                                       k_stack[b.par][r0:r0 + rows, i, ch * P:(ch + 1) * P],
                                       q_stack[b.par][r0:r0 + rows, i, :], start=True, stop=True, skip_group_check=masked)
                        if masked:
                            for t in range(QT):
                                mm = pe.matmul(st_bank[:, j, cc * S + t * P:cc * S + (t + 1) * P],
                                               maskb[b.par][:, t, ch * P:(ch + 1) * P], eye_b[:, :],
                                               start=False, stop=True, skip_group_check=True)
                        if cc == 1:
                            mm.then_inc(st_mm, 1)

            def values(b, g):
                pe.wait_ge(probs_ready, count(b, 2 * UNITS, 8 * (g + 1)))
                if g == 0:
                    pe.wait_ge(v_ready, count(b, 1, 1))
                if g % 2 == 0 and not (b.first and g == 0):
                    pe.wait_ge(att_ready, count(b, 2, g // 2))
                for ch in range(KC):
                    for jj in range(4):
                        unit = 2 * (jj // 2) + ch // 2
                        cc = ch % 2
                        mm = pe.matmul(av_bank[VW * jj:VW * (jj + 1), (g % 2) * S:(g % 2 + 1) * S],
                                       v_sb[b.par][:, ch, 4 * g + jj, :],
                                       probs[:, g % 2, unit, jj % 2, cc * S:(cc + 1) * S],
                                       start=(ch == 0), stop=(ch == KC - 1), skip_group_check=True)
                mm.then_inc(av_mm, 1)

            def transpose_heads(n, hh, a, b, c):
                pe.wait_ge(att_ready, count(n, 2, hh + 1))
                if hh == 1 and b:
                    pe.wait_ge(neg_maxT_ready, count(b, 2, 2))
                if hh == 1:
                    pe.wait_ge(att_n_ready, count(n, 2, 1))
                if hh == 0 and c:
                    pe.wait_ge(acc_set, count(c, 1, 1))
                if hh == 0 and a:
                    pe.wait_ge(neg_maxT_ready, count(a, 2, 1))
                for t in range(QT):
                    for gl in range(2):
                        k = 2 * t + gl
                        mm = pe.transpose(misc[:, k * P:(k + 1) * P], att_sb[:, gl, t * P:(t + 1) * P], eye_f[:, :])
                mm.then_inc(attT_mm, 1)

            def transpose_normed(c, p):
                pe.wait_ge(att_n_ready, count(c, 2, 2))
                if p:
                    pe.wait_ge(xnT_ready, count(p, 1, 1))
                for t in range(QT):
                    mm = pe.transpose(misc[:, t * P:(t + 1) * P], att_n[:, t, :], eye_f[:, :])
                mm.then_inc(att_nT_mm, 1)

            def project_out(c, p):
                pe.wait_ge(att_nT_ready, count(c, 1, 1))
                if c.first:
                    pe.wait_ge(ffn_in, 16 * 7)
                if p:
                    pe.wait_ge(q_rest_ready, count(p, 1, 1))
                for t in range(QT):
                    mm = pe.matmul(misc[:, t * P:(t + 1) * P], att_nT[:, t * P:(t + 1) * P], wo_sb[:, :],
                                   start=True, stop=True)
                mm.then_inc(proj_mm, 1)

            def transpose_x2(c, p):
                pe.wait_ge(xn2_ready, count(c, 1, 1))
                if p:
                    pe.wait_ge(k_rest_ready, count(p, 1, 1))
                for t in range(QT):
                    mm = pe.transpose(misc[:, t * P:(t + 1) * P], xn2[:, t, :], eye_f[:, :])
                mm.then_inc(xn2T_mm, 1)

            def gate(c):
                pe.wait_ge(xn2T_ready, count(c, 1, 1))
                for t in range(QT):
                    mm = pe.matmul(misc[:, t * E:(t + 1) * E], xn2T[c.par][:, t * P:(t + 1) * P], wg_sb[:, :],
                                   start=True, stop=True)
                mm.then_inc(logits_mm, 1)

            def transpose_route(c, a):
                pe.wait_ge(route_ready, count(c, 1, 1))
                if a:
                    pe.wait_ge(neg_maxT_ready, count(a, 2, 1))
                for t in range(QT):
                    mm = pe.transpose(misc[0:E, t * P:(t + 1) * P], route_w[:, t, :], eye_f[:, :])
                mm.then_inc(routeT_mm, 1)

            def bias2(c):
                pe.wait_ge(routeT_ready, count(c, 1, 1))
                for t in range(QT):
                    mm = pe.matmul(misc[:, t * P:(t + 1) * P], route_wT[:, t * P:(t + 1) * P], b2_sb[:, :],
                                   start=True, stop=True)
                mm.then_inc(b2_mm, 1)

            def hidden(c, x_):
                if not (c.first and x_ == 0):
                    pe.wait_ge(h_ready, count(c, 2 * E, 2 * x_))
                for ch in range(HC):
                    mm = pe.matmul(h_bank[:, ch * S:(ch + 1) * S], w1_sb[:, x_, ch * P:(ch + 1) * P], xn2T[c.par][:, :],
                                   start=True, stop=True)
                mm.then_inc(h_mm, 1)

            def expert_out(c, p):
                pe.wait_ge(h_ready, count(c, 2 * E, 4 * p + 4))
                if not (c.first and p == 0):
                    pe.wait_ge(acc_step, count(c, 2 * E, 4 * p))
                for el in range(2):
                    for t in range(QT):
                        k = 2 * el + t
                        for ch in range(HC):
                            mm = pe.matmul(y_bank[:, k * P:(k + 1) * P],
                                           h_sb[:, (2 * p + el) % 4, ch, t * P:(t + 1) * P],
                                           w2_sb[:, 2 * p + el, ch, :], start=(ch == 0), stop=(ch == HC - 1))
                mm.then_inc(y_mm, 1)

            def step_of(masked):
                def step(p, a, b, c, d):
                    for slot in range(UNITS):
                        late = slot < UNITS // 2
                        x_batch = d if late else c
                        if b:
                            scores(b, slot, masked)
                        if slot == 0:
                            if c:
                                values(c, 3)
                            if b:
                                transpose_max(b, 1, c)
                        if c and slot == 1:
                            transpose_heads(c, 1, a, b, None)
                        if p and slot == 2:
                            transpose_x(p, a, b, c)
                        if c and slot == 3:
                            transpose_normed(c, p)
                        if p and slot == 4:
                            project_q(p, c)
                        if c and slot == 5:
                            project_out(c, p)
                        if p and slot == 6:
                            project_k(p, c)
                        if c and slot == 7:
                            transpose_x2(c, p)
                        if a:
                            max_scores(a, slot, masked)
                        if c and slot == 8:
                            gate(c)
                        if a and slot == 9:
                            project_v(a, p, c)
                        if a and slot == 10:
                            transpose_max(a, 0, c)
                        if c and slot == 11:
                            transpose_route(c, a)
                        if c and slot == 12:
                            bias2(c)
                        if b and slot == 13:
                            transpose_heads(b, 0, a, None, c)
                        if b and slot in (5, 9, 13):
                            values(b, (slot - 5) // 4)
                        if slot in OUT_SLOTS and (c if slot > OUT_NEXT else d):
                            expert_out(c if slot > OUT_NEXT else d, OUT_SLOTS[slot])
                        if x_batch and slot in HIDDEN_SLOTS:
                            hidden(x_batch, HIDDEN_SLOTS[slot])
                return step

            first_step(step_of(False))
            pe.wait_ge(any_col_set, 1)
            pe.wait_ge(k_rest_ready, 1)
            pe.transpose(misc[0:1, 0:P], any_col[:, :], eye_f[:, :]).then_inc(any_mm, 1)
            pe.wait_ge(any_flag_set, 1)
            any_masked = pe.value_load(any_flag[0:1, 0:1])
            with pe.If(any_masked > 0):
                later_steps(pe, step_of(True))
            with pe.Else():
                later_steps(pe, step_of(False))

        @block.scalar
        def _(act):
            act.wait_ge(ffn_in, 16)
            act.activation(gate_t[:, :], gates_sb[:, :], ACT.Tanh).then_inc(gates_set, 1)

            def copy_xnT(a):
                act.wait_ge(xnT_mm, count(a, 1, 1))
                act.copy(xnT[:, :], misc[:, 0:S]).then_inc(xnT_ready, 1)

            def high_part(a, mm, written, parts, width, ready):
                act.wait_ge(mm, count(a, 1, 1))
                if not a.first:
                    act.wait_ge(written, count(a, 16, 0))
                act.copy(parts[:, 0, :], misc[:, 0:width]).then_inc(ready, 1)

            def copy_v(a):
                act.wait_ge(v_mm, count(a, 1, 1))
                if a.first:
                    act.wait_ge(v_filled, 4)
                if not a.early:
                    act.wait_ge(av_mm, count(a, 4, -4))
                act.copy(v_sb[a.par][:, :, :, 0:DK].rearrange("p c h d -> p (c h) d"),
                         misc[:, :].rearrange("p (c d) -> p c d", d=DK)).then_inc(v_ready, 1)

            def exps(b, u):
                g = u // 4
                for j in range(2):
                    act.wait_ge(st_mm, count(b, 2 * UNITS, 2 * u + j + 1))
                    if j == 0 and u % 4 == 0 and not (b.first and g < 2):
                        act.wait_ge(av_mm, count(b, 4, g - 1))
                    act.activation(probs[:, g % 2, u % 4, j, :], st_bank[:, j, :], ACT.Exp, scale=SCALE
                                   ).then_inc(probs_ready, 1)

            def copy_heads(b, hh):
                act.wait_ge(av_mm, count(b, 4, 2 * hh + 2))
                if not (b.first and hh == 0):
                    act.wait_ge(attT_mm, count(b, 2, hh))
                act.copy(att_sb[:, :, :].rearrange("p g s -> p (g s)"), av_bank[:, :]).then_inc(att_ready, 1)

            def copy_normed(c):
                act.wait_ge(att_nT_mm, count(c, 1, 1))
                act.copy(att_nT[:, :], misc[:, 0:S]).then_inc(att_nT_ready, 1)

            def copy_x2T(c):
                act.wait_ge(xn2T_mm, count(c, 1, 1))
                act.copy(xn2T[c.par][:, :], misc[:, 0:S]).then_inc(xn2T_ready, 1)

            def route_exp(c):
                act.wait_ge(logits_read, count(c, 1, 1))
                act.activation(expert_e[:, :, :], logit_d[:, :, :], ACT.Exp).then_inc(expert_e_ready, 1)

            def copy_routeT(c):
                act.wait_ge(routeT_mm, count(c, 1, 1))
                act.copy(route_wT[:, :], misc[0:E, 0:S]).then_inc(routeT_ready, 1)

            def set_acc(c):
                act.wait_ge(b2_mm, count(c, 1, 1))
                if not c.first:
                    act.wait_ge(out_ready, count(c, 1, 0))
                act.copy(acc[:, :, :].rearrange("p t d -> p (t d)"), misc[:, 0:S]).then_inc(acc_set, 1)

            def relu(c, x_):
                if x_ % 2 == 0 and not (c.first and x_ < 4):
                    act.wait_ge(y_mm, count(c, 4, x_ // 2 - 1))
                act.wait_ge(h_mm, count(c, E, x_ + 1))
                for ch in range(HC):
                    act.activation(h_sb[:, x_ % 4, ch, :], h_bank[:, ch * S:(ch + 1) * S], ACT.Relu,
                                   bias=b1_sb[:, x_, ch:ch + 1]).then_inc(h_ready, 1)

            def step(p, a, b, c, d):
                for slot in range(UNITS):
                    x_batch = d if slot < UNITS // 2 else c
                    if b:
                        exps(b, slot)
                    if c and slot == 0:
                        copy_heads(c, 1)
                    if p and slot == 2:
                        copy_xnT(p)
                    if c and slot == 3:
                        copy_normed(c)
                    if p and slot == 4:
                        high_part(p, q_mm, q_scratch_out, q_parts, S, q1_ready)
                    if p and slot == 6:
                        high_part(p, k_mm, k_scratch_out, k_parts, S2, k1_ready)
                    if c and slot == 7:
                        copy_x2T(c)
                    if c and slot == 8:
                        route_exp(c)
                    if a and slot == 9:
                        copy_v(a)
                    if b and slot == 10:
                        copy_heads(b, 0)
                    if c and slot == 11:
                        copy_routeT(c)
                    if c and slot == 12:
                        set_acc(c)
                    if x_batch and slot in HIDDEN_SLOTS:
                        relu(x_batch, HIDDEN_SLOTS[slot])

            first_step(step)
            act.wait_ge(ffn_in, 16 * 7)
            later_steps(act, step)

        @block.vector
        def _(dve):
            def statistics(n, step_sem):
                for t in range(QT):
                    dve.bn_stats(ln_stats[:, t, :], x_all[:, bass.ds(2 * n.n + t, 1), :].rearrange("p t d -> p (t d)")
                                 ).then_inc(step_sem, 1)
                hold(dve, step_sem, count(n, 5, 2))
                for t in range(QT):
                    dve.bn_aggr(ln_mv[:, t, :], ln_stats[:, t, :]).then_inc(step_sem, 1)
                dve.wait_ge(step_sem, count(n, 5, 4))
                dve.tensor_scalar(var_eps[:, :], ln_mv[:, :, 1], EPS, None, ALU.add).then_inc(step_sem, 1)

            def layernorm(n, rstd_ready, rstd, dst, dst_free, ready):
                dve.wait_ge(rstd_ready, count(n, 1, 1))
                if not n.first:
                    dve.wait_ge(dst_free, count(n, 1, 0))
                for t in range(QT):
                    ln = dve.tensor_scalar(dst[:, t, :], x_all[:, bass.ds(2 * n.n + t, 1), :].rearrange("p t d -> p (t d)"),
                                           ln_mv[:, t, 0:1], rstd[:, t:t + 1], ALU.subtract, ALU.mult)
                ln.then_inc(ready, 1)

            def rest(a, high, parts, dst, width, low, ready):
                dve.wait_ge(high, count(a, 1, 1))
                if not a.first:
                    dve.wait_ge(low, count(a, 2, 0))
                dve.tensor_tensor(dst[:, :], misc[:, 0:width], parts[:, 0, :], ALU.subtract).then_inc(ready, 1)

            def reduce_max(a, v):
                i, qt = MX_UNITS[v]
                dve.wait_ge(mx_mm, count(a, UNITS, v + 1))
                dve.tensor_reduce(row_max[:, qt, :, i], mx_bank[:, :, :], AX_X, ALU.max).then_inc(mx_read, 1)

            def negate_max(a, half):
                dve.wait_ge(mx_read, count(a, UNITS, UNITS // 2 * (half + 1)))
                pairs = slice(half * HALF, (half + 1) * HALF)
                dve.tensor_scalar(neg_max[:, :, :, :], row_max[:, :, :, pairs], LOWEST, -1.0, ALU.max, ALU.mult
                                  ).then_inc(neg_max_step, 1)
                dve.wait_ge(neg_max_step, count(a, 6, 3 * half + 1))
                if not (a.first and half == 0):
                    dve.wait_ge(neg_max_mm, count(a, 2, half))
                src = neg_max[:, :, :, :].rearrange("p t j i -> p t (j i)")
                dve.tensor_copy(neg_max_parts[:, :, 0, :], src).then_inc(neg_max_step, 1)
                dve.wait_ge(neg_max_step, count(a, 6, 3 * half + 2))
                dve.tensor_tensor(neg_max_parts[:, :, 1, :], src, neg_max_parts[:, :, 0, :], ALU.subtract
                                  ).then_inc(neg_max_step, 1)

            def copy_maxT(n, half):
                dve.wait_ge(neg_max_mm, count(n, 2, half + 1))
                if not (n.first and half == 0):
                    dve.wait_ge(max_scratch_out, count(n, 32, 16 * half))
                dve.tensor_copy(neg_maxT[:, :], misc[:, :].bitcast(BF16)[0:M_ROWS * 2 * HALF, 0:S]
                                ).then_inc(neg_maxT_ready, 1)

            def normalise(b, hh):
                dve.wait_ge(attT_mm, count(b, 2, hh + 1))
                heads = misc[:, :].rearrange("p (k w) -> p k w", w=VW)
                dve.tensor_scalar(den[:, :], heads[:, :, DK], 1e-30, None, ALU.max).then_inc(den_step, 1)
                dve.wait_ge(den_step, count(b, 4, 2 * hh + 1))
                dve.reciprocal(rden[:, :], den[:, :]).then_inc(den_step, 1)
                dve.wait_ge(den_step, count(b, 4, 2 * hh + 2))
                if hh == 0 and not b.first:
                    dve.wait_ge(att_nT_mm, count(b, 1, 0))
                half = H // 2
                dve.tensor_tensor(
                    att_n[:, :, hh * 64:(hh + 1) * 64].rearrange("p t (h d) -> p t h d", d=DK),
                    misc[:, :].rearrange("p (t h w) -> p t h w", t=QT, h=half)[:, :, :, 0:DK],
                    rden[:, :].rearrange("p (t h) -> p t h", t=QT).unsqueeze(3).to_broadcast([P, QT, half, DK]),
                    ALU.mult).then_inc(att_n_ready, 1)

            def residual(c):
                dve.wait_ge(proj_mm, count(c, 1, 1))
                if c.first:
                    dve.wait_ge(gates_set, 1)
                xt = x_all[:, c.tiles(), :]
                dve.scalar_tensor_tensor(out=xt, in0=misc[:, 0:S].rearrange("p (t d) -> p t d", t=QT),
                                         scalar=gate_t[:, 0:1], in1=xt, op0=ALU.mult, op1=ALU.add).then_inc(x2_ready, 1)
                hold(dve, x2_ready, count(c, 1, 1))

            def logits(c):
                hold(dve, logits_mm, count(c, 1, 1))
                lg = misc[:, 0:QT * E].rearrange("p (t e) -> p t e", t=QT)
                for t in range(QT):
                    dve.max(logit_top[:, t, :], lg[:, t, :]).then_inc(logits_step, 1)
                dve.wait_ge(logits_step, count(c, 2, 2))
                dve.tensor_tensor(logit_d[:, :, :], lg, logit_top[:, :, 0:1].to_broadcast([P, QT, E]), ALU.subtract
                                  ).then_inc(logits_read, 1)

            def route(c):
                k = [0]

                def link(ins, need=True):
                    k[0] += 1
                    ins.then_inc(route_step, 1)
                    if need:
                        hold(dve, route_step, count(c, ROUTE_STEPS, k[0]))

                dve.wait_ge(expert_e_ready, count(c, 1, 1))
                link(dve.tensor_reduce(expert_sum[:, :], expert_e[:, :, :], AX_X, ALU.add))
                link(dve.reciprocal(expert_inv[:, :], expert_sum[:, :]))
                link(dve.tensor_tensor(expert_p[:, :, :], expert_e[:, :, :],
                                       expert_inv[:, :].unsqueeze(2).to_broadcast([P, QT, E]), ALU.mult))
                for t in range(QT):
                    top = dve.max(top_p[:, t, :], expert_p[:, t, :])
                link(top)
                for t in range(QT):
                    top = dve.max_index(top_i[:, t, :], top_p[:, t, :], expert_p[:, t, :])
                link(top)
                link(dve.tensor_copy(top_f[:, :, :], top_i[:, :, 0:2]))
                for m in range(2):
                    link(dve.tensor_tensor(is_top[:, m, :, :], expert_no[:, :, :],
                                           top_f[:, :, m:m + 1].to_broadcast([P, QT, E]), ALU.is_equal), m == 1)
                link(dve.tensor_tensor(chosen[:, :, :], is_top[:, 0, :, :], is_top[:, 1, :, :], ALU.add))
                if not c.first:
                    dve.wait_ge(routeT_mm, count(c, 1, 0))
                assert k[0] == ROUTE_STEPS
                dve.tensor_tensor(route_w[:, :, :], chosen[:, :, :], expert_p[:, :, :], ALU.mult
                                  ).then_inc(route_ready, 1)

            def add_experts(c, p):
                dve.wait_ge(y_mm, count(c, 4, p + 1))
                for el in range(2):
                    x_ = 2 * p + el
                    if x_ == 0:
                        dve.wait_ge(acc_set, count(c, 1, 1))
                        dve.wait_ge(route_ready, count(c, 1, 1))
                    else:
                        dve.wait_ge(acc_step, count(c, 2 * E, 2 * x_))
                    for t in range(QT):
                        k = 2 * el + t
                        dve.scalar_tensor_tensor(out=acc[:, t, :], in0=y_bank[:, k * P:(k + 1) * P],
                                                 scalar=route_w[:, t, x_:x_ + 1], in1=acc[:, t, :],
                                                 op0=ALU.mult, op1=ALU.add).then_inc(acc_step, 1)

            def finish(d):
                dve.wait_ge(acc_step, count(d, 2 * E, 2 * E))
                xt = x_all[:, d.tiles(), :]
                dve.scalar_tensor_tensor(out=xt, in0=acc[:, :, :], scalar=gate_t[:, 1:2], in1=xt,
                                         op0=ALU.mult, op1=ALU.add).then_inc(out_ready, 1)

            def step(p, a, b, c, d):
                for slot in range(UNITS):
                    if b and slot == 0:
                        copy_maxT(b, 1)
                    if p and slot == 0:
                        statistics(p, ln1_step)
                    if p and slot == 1:
                        layernorm(p, rstd1_ready, rstd1, xn, xnT_mm, xn_ready)
                    if c and slot == 1:
                        normalise(c, 1)
                    if p and slot == 4:
                        rest(p, q1_ready, q_parts, q_rest, S, q_low_ready, q_rest_ready)
                    if c and slot == 5:
                        residual(c)
                        statistics(c, ln2_step)
                    if p and slot == 6:
                        rest(p, k1_ready, k_parts, k_rest, S2, k_low_ready, k_rest_ready)
                    if c and slot == 6:
                        layernorm(c, rstd2_ready, rstd2, xn2, xn2T_mm, xn2_ready)
                    if a:
                        reduce_max(a, slot)
                    if a and slot == 8:
                        negate_max(a, 0)
                    if c and slot == 8:
                        logits(c)
                    if slot in ADD_SLOTS and (c if slot > OUT_NEXT else d):
                        add_experts(c if slot > OUT_NEXT else d, ADD_SLOTS[slot])
                    if d and slot == 9:
                        finish(d)
                    if c and slot == 9:
                        route(c)
                    if a and slot == 10:
                        copy_maxT(a, 0)
                    if b and slot == 13:
                        normalise(b, 0)
                    if a and slot == 15:
                        negate_max(a, 1)

            dve.wait_ge(x_in, 16)
            first_step(step)
            dve.wait_ge(mask_in, 16)
            dve.tensor_reduce(any_col[:, :], mask_all[:, :, :].rearrange("p t k -> p (t k)").bitcast(I32), AX_X, ALU.max
                              ).then_inc(any_col_set, 1)
            dve.wait_ge(any_mm, 1)
            dve.tensor_reduce(any_row[:, :], misc[0:1, 0:P], AX_X, ALU.max).then_inc(any_row_set, 1)
            dve.wait_ge(any_row_set, 1)
            dve.tensor_scalar(any_flag[:, :], any_row[:, :], 1.0, None, ALU.min).then_inc(any_flag_set, 1)
            dve.wait_ge(x_rest_in, 16)
            dve.wait_ge(numbers_set, 1)
            later_steps(dve, step)


def kernel(x, ctx_1024, mask_BxSxS2_bf0, g_xattn, g_ffn, L0_xattn_W_Q, L0_xattn_W_K, L0_xattn_W_V, L0_xattn_W_O,
           L0_ffn_Wg, L0_ffn_W1, L0_ffn_b1, L0_ffn_W2, L0_ffn_b2):
    import numpy as np
    import concourse.bacc as bacc
    from concourse.bass_utils import run_bass_kernel_spmd

    def pair_order(w):
        return np.ascontiguousarray(np.asarray(w).T.reshape(D, PAIRS, 2, DK).transpose(0, 2, 1, 3).reshape(D, D))

    arrays = {
        "x": np.asarray(x),
        "ctxT": np.ascontiguousarray(np.asarray(ctx_1024).transpose(0, 2, 1)),
        "mask": np.asarray(mask_BxSxS2_bf0),
        "gates": np.ascontiguousarray(np.broadcast_to(
            np.concatenate([np.asarray(g_xattn), np.asarray(g_ffn)])[None, :], (P, 2))),
        "wqT": pair_order(L0_xattn_W_Q),
        "wkT": pair_order(L0_xattn_W_K),
        "wvT": np.ascontiguousarray(np.asarray(L0_xattn_W_V).T),
        "woT": np.ascontiguousarray(np.asarray(L0_xattn_W_O).T),
        "wg": np.asarray(L0_ffn_Wg),
        "w1": np.ascontiguousarray(np.asarray(L0_ffn_W1).transpose(1, 0, 2)),
        "b1": np.ascontiguousarray(np.asarray(L0_ffn_b1).reshape(E, HC, P).transpose(2, 0, 1)),
        "w2": np.ascontiguousarray(np.asarray(L0_ffn_W2).reshape(E, HC, P, D).transpose(2, 0, 1, 3)),
        "b2": np.asarray(L0_ffn_b2),
        "eye": np.eye(P, dtype=np.float32),
    }
    nc = bacc.Bacc("TRN2", target_bir_lowering=False, num_devices=1)
    args = {name: nc.dram_tensor(f"in_{name}", a.shape, mybir.dt.from_np(a.dtype), kind="ExternalInput").ap()
            for name, a in arrays.items()}
    result = nc.dram_tensor("out_0", (B, S, D), F32, kind="ExternalOutput").ap()
    build(nc, out=result, **args)
    run = run_bass_kernel_spmd(nc, [{f"in_{name}": a for name, a in arrays.items()}], core_ids=[0])
    return run.results[0]["out_0"]
```

```python
from contextlib import ExitStack

import concourse.bass as bass
from concourse import mybir

F32 = mybir.dt.float32
BF16 = mybir.dt.bfloat16
U8 = mybir.dt.uint8
U32 = mybir.dt.uint32
I32 = mybir.dt.int32
ALU = mybir.AluOpType
ACT = mybir.ActivationFunctionType
AX_X = mybir.AxisListType.X

P = 128
B = 8
S = 256
S2 = 512
D = 128
H = 16
DK = D // H
QT = S // P
KC = S2 // P
PAIRS = H // 2
E = 8
HC = 2
VW = 32
UNITS = 2 * PAIRS
GROUPS = 4
SCALE = 1.0 / float(DK) ** 0.5
EPS = 1e-5
MASKED = -1e30
TWO_ONES = 1.0 + 0x3F80 * 2.0 ** -23
LOWEST = -1e29

Q_RUNS = [(0, 3, 1), (0, 2, 1), (0, 1, 1)]
K_RUNS = [(0, 1, 3), (1, 1, 2), (2, 1, 1)]
TERMS = 6
QK_ROWS = TERMS * DK
M_ROWS = 2
SCRATCH_DMAS = len(Q_RUNS)
STACK_DMAS = 2 * 2
MAX_DMAS = 2
HALF = PAIRS // 2

MX_UNITS = [(i, qt) for i in range(PAIRS) for qt in range(QT)]
HIDDEN_SLOTS = {11 + 2 * x: x for x in range(3)}
LATER_HIDDEN_SLOTS = {2 * x - 5: x for x in range(3, E)}
OUT_SLOTS = {14: 0}
LATER_OUT_SLOTS = {2 * x - 2: x for x in range(1, E)}
ADD_SLOTS = {4 * p + 1: p for p in range(E // 2)}
ROUTE_STEPS = 9


class Batch:

    def __init__(self, r, off):
        self.n = 2 * r + off
        self.turn = r + off // 2
        self.par = off % 2
        self.first = isinstance(self.n, int) and self.n == 0
        self.third = isinstance(self.n, int) and self.n == 2
        self.early = isinstance(self.n, int) and self.n < 2

    def tiles(self):
        return bass.ds(2 * self.n, QT)


def count(batch, per, k):
    return per * batch.n + k


def hold(engine, semaphore, value):
    engine.wait_ge(semaphore, value)
    engine.nop(nofuse=True)


def first_steps(step, between=None):
    step(Batch(0, 0), None, None, None, None)
    if between:
        between()
    step(Batch(0, 1), None, None, None, None)


def later_steps(engine, step):
    def at(r, off):
        return tuple(Batch(r, off + k) if not isinstance(r, int) or 0 <= off + k < B else None for k in (2, 1, 0, -1, -2))

    step(None, Batch(0, 0), None, None, None)
    for s in (0, 1):
        step(*at(0, s))
    with engine.Fori(0, 2) as r:
        step(*at(r, 2))
        step(*at(r, 3))
    for s in (6, 7, 8, 9):
        step(*at(0, s))


def build(nc, x, ctxT, mask, gates, wqT, wkT, wvT, woT, wg, w1, b1, w2, b2, eye, out):
    with ExitStack() as stack:
        def sb(name, shape, dt):
            return stack.enter_context(nc.sbuf_tensor(name, shape, dt))

        def sem(name):
            return stack.enter_context(nc.semaphore(name))

        x_all = sb("x_all", [P, B * QT, D], F32)
        mask_all = sb("mask_all", [P, B * QT, S2], U8)
        mask_sb = [sb(f"mask_sb{p}", [P, QT, S2], U8) for p in range(2)]
        ctx_sb = [sb(f"ctx_sb{p}", [P, S2], F32) for p in range(2)]
        maskb = [sb(f"maskb{p}", [P, QT, S2], BF16) for p in range(2)]
        k_stack = [sb(f"k_stack{p}", [P, PAIRS, S2], BF16) for p in range(2)]
        q_stack = [sb(f"q_stack{p}", [P, PAIRS, S], BF16) for p in range(2)]
        v_sb = [sb(f"v_sb{p}", [P, KC, H, VW], F32) for p in range(2)]
        k_parts = sb("k_parts", [P, 3, S2], BF16)
        q_parts = sb("q_parts", [P, 3, S], BF16)
        k_rest = sb("k_rest", [P, S2], F32)
        q_rest = sb("q_rest", [P, S], F32)
        probs = sb("probs", [P, 2, 4, 2, 2 * S], F32)
        eye_f = sb("eye_f", [P, P], F32)
        eye_b = sb("eye_b", [P, P], BF16)
        wq_sb = sb("wq_sb", [P, D], F32)
        wk_sb = sb("wk_sb", [P, D], F32)
        wv_sb = sb("wv_sb", [P, D], F32)
        wo_sb = sb("wo_sb", [P, D], F32)
        wg_sb = sb("wg_sb", [P, E], F32)
        w1_sb = sb("w1_sb", [P, E, HC * P], F32)
        w2_sb = sb("w2_sb", [P, E, HC, D], F32)
        b1_sb = sb("b1_sb", [P, E, HC], F32)
        b2_sb = sb("b2_sb", [E, D], F32)
        gates_sb = sb("gates_sb", [P, 2], F32)
        gate_t = sb("gate_t", [P, 2], F32)
        ln_stats = sb("ln_stats", [P, QT, 6], F32)
        ln_mv = sb("ln_mv", [P, QT, 2], F32)
        var_eps = sb("var_eps", [P, QT], F32)
        minus_half = sb("minus_half", [P, QT], F32)
        rstd1 = sb("rstd1", [P, QT], F32)
        rstd2 = sb("rstd2", [P, QT], F32)
        xn = sb("xn", [P, QT, D], F32)
        xnT = sb("xnT", [P, S], F32)
        xn2 = sb("xn2", [P, QT, D], F32)
        xn2T = [sb(f"xn2T{p}", [P, S], F32) for p in range(2)]
        row_max = sb("row_max", [P, QT, 2, PAIRS], F32)
        neg_max = sb("neg_max", [P, QT, 2, HALF], F32)
        neg_max_parts = sb("neg_max_parts", [P, QT, M_ROWS, 2 * HALF], BF16)
        neg_maxT = sb("neg_maxT", [M_ROWS * 2 * HALF, S], BF16)
        att_sb = sb("att_sb", [P, 2, S], F32)
        den = sb("den", [P, 16], F32)
        rden = sb("rden", [P, 16], F32)
        att_n = sb("att_n", [P, QT, D], F32)
        att_nT = sb("att_nT", [P, S], F32)
        h_sb = sb("h_sb", [P, 4, HC, S], F32)
        acc = [sb(f"acc{p}", [P, QT, D], F32) for p in range(2)]
        logit_top = sb("logit_top", [P, QT, 8], F32)
        logit_d = sb("logit_d", [P, QT, E], F32)
        expert_e = sb("expert_e", [P, QT, E], F32)
        expert_sum = sb("expert_sum", [P, QT], F32)
        expert_inv = sb("expert_inv", [P, QT], F32)
        expert_p = sb("expert_p", [P, QT, E], F32)
        top_p = sb("top_p", [P, QT, 8], F32)
        top_i = sb("top_i", [P, QT, 8], U32)
        top_f = sb("top_f", [P, QT, 2], F32)
        is_top = sb("is_top", [P, 2, QT, E], F32)
        chosen = sb("chosen", [P, QT, E], F32)
        expert_no = sb("expert_no", [P, QT, E], F32)
        route_w = [sb(f"route_w{p}", [P, QT, E], F32) for p in range(2)]
        route_wT = sb("route_wT", [E, S], F32)
        any_col = sb("any_col", [P, 1], F32)
        any_row = sb("any_row", [1, 1], F32)
        any_flag = sb("any_flag", [1, 1], I32)

        bank = [stack.enter_context(nc.psum_tensor(f"bank{i}", [P, 512], F32)) for i in (4, 7)]
        st_bank = stack.enter_context(nc.psum_tensor("st_bank", [P, 2, 512], F32))
        mx_bank = stack.enter_context(nc.psum_tensor("mx_bank", [P, 2, 512], F32))
        ffn_bank = stack.enter_context(nc.psum_tensor("ffn_bank", [P, 2, 512], F32))
        av_bank, misc = bank
        h_bank, y_bank = ffn_bank[:, 0, :], ffn_bank[:, 1, :]

        k_scratch = nc.dram_tensor("k_scratch", [2, TERMS, 2, DK, PAIRS, S2], BF16, kind="Internal").ap()
        q_scratch = nc.dram_tensor("q_scratch", [2, TERMS, 2, DK, PAIRS, S], BF16, kind="Internal").ap()

        max_scratch = nc.dram_tensor("max_scratch", [2, 2, M_ROWS * 2 * HALF, S], BF16, kind="Internal").ap()

        x_in = sem("x_in")
        x_second_in = sem("x_second_in")
        x_rest_in = sem("x_rest_in")
        eye_in = sem("eye_in")
        wq_in = sem("wq_in")
        wk_in = sem("wk_in")
        wv_in = sem("wv_in")
        gates_in = sem("gates_in")
        mask_in = sem("mask_in")
        ffn_in = sem("ffn_in")
        batch_mask_in = [sem(f"batch_mask_in{p}") for p in range(2)]
        ctx_in = [sem(f"ctx_in{p}") for p in range(2)]
        max_scratch_out = sem("max_scratch_out")
        q_scratch_out = sem("q_scratch_out")
        k_scratch_out = sem("k_scratch_out")
        stack_in = [[sem(f"stack_in{p}_{half}") for half in range(2)] for p in range(2)]
        neg_max_in = [[sem(f"neg_max_in{p}_{half}") for half in range(2)] for p in range(2)]
        out_done = sem("out_done")
        stack_ones = sem("stack_ones")
        v_filled = sem("v_filled")
        numbers_set = sem("numbers_set")
        eye_b_set = sem("eye_b_set")
        half_set = sem("half_set")
        gates_set = sem("gates_set")
        any_col_set = sem("any_col_set")
        any_mm = sem("any_mm")
        any_row_set = sem("any_row_set")
        any_flag_set = sem("any_flag_set")
        ln1_step = sem("ln1_step")
        rstd1_ready = sem("rstd1_ready")
        xn_ready = sem("xn_ready")
        xnT_mm = sem("xnT_mm")
        xnT_ready = sem("xnT_ready")
        q_mm = sem("q_mm")
        k_mm = sem("k_mm")
        v_mm = sem("v_mm")
        q1_ready = sem("q1_ready")
        q_rest_ready = sem("q_rest_ready")
        q_low_ready = sem("q_low_ready")
        k1_ready = sem("k1_ready")
        k_rest_ready = sem("k_rest_ready")
        k_low_ready = sem("k_low_ready")
        v_ready = sem("v_ready")
        maskb_ready = sem("maskb_ready")
        mx_mm = sem("mx_mm")
        mx_read = sem("mx_read")
        neg_max_step = sem("neg_max_step")
        neg_max_mm = sem("neg_max_mm")
        neg_maxT_ready = sem("neg_maxT_ready")
        st_mm = sem("st_mm")
        probs_ready = sem("probs_ready")
        av_mm = sem("av_mm")
        att_ready = sem("att_ready")
        attT_mm = sem("attT_mm")
        den_step = sem("den_step")
        att_n_ready = sem("att_n_ready")
        att_nT_mm = sem("att_nT_mm")
        att_nT_ready = sem("att_nT_ready")
        proj_mm = sem("proj_mm")
        x2_ready = sem("x2_ready")
        ln2_step = sem("ln2_step")
        rstd2_ready = sem("rstd2_ready")
        xn2_ready = sem("xn2_ready")
        xn2T_mm = sem("xn2T_mm")
        xn2T_ready = sem("xn2T_ready")
        logits_mm = sem("logits_mm")
        logits_step = sem("logits_step")
        logits_read = sem("logits_read")
        expert_e_ready = sem("expert_e_ready")
        route_step = sem("route_step")
        route_ready = sem("route_ready")
        routeT_mm = sem("routeT_mm")
        routeT_ready = sem("routeT_ready")
        b2_mm = sem("b2_mm")
        acc_set = sem("acc_set")
        h_mm = sem("h_mm")
        h_ready = sem("h_ready")
        y_mm = sem("y_mm")
        acc_step = sem("acc_step")
        out_ready = sem("out_ready")

        block = stack.enter_context(nc.Block())

        @block.sync
        def _(sp):
            x_tiles = x.rearrange("b (t p) d -> p (b t) d", p=P)

            mask_tiles = mask.rearrange("b (t p) k -> p (b t) k", p=P)

            def load_ctx(n):
                if not n.early:
                    hold(sp, v_mm, count(n, 1, -1))
                sp.dma_start(ctx_sb[n.par][:, :], ctxT[bass.ds(n.n, 1)].rearrange("b d k -> d (b k)")
                             ).then_inc(ctx_in[n.par], 16)

            def load_mask(n):
                if not n.early:
                    hold(sp, maskb_ready, count(n, 1, -1))
                sp.dma_start(mask_sb[n.par][:, :, :], mask_tiles[:, n.tiles(), :]).then_inc(batch_mask_in[n.par], 16)

            sp.dma_start(x_all[:, 0:QT, :], x_tiles[:, 0:QT, :]).then_inc(x_in, 16)
            sp.dma_start(eye_f[:, :], eye).then_inc(eye_in, 16)
            sp.dma_start(wq_sb[:, :], wqT).then_inc(wq_in, 16)
            load_ctx(Batch(0, 0))
            sp.dma_start(wk_sb[:, :], wkT).then_inc(wk_in, 16)
            sp.dma_start(wv_sb[:, :], wvT).then_inc(wv_in, 16)
            sp.dma_start(x_all[:, QT:2 * QT, :], x_tiles[:, QT:2 * QT, :]).then_inc(x_second_in, 16)
            load_ctx(Batch(0, 1))
            sp.dma_start(mask_all[:, :, :], mask_tiles).then_inc(mask_in, 16)
            for n in range(2):
                load_mask(Batch(0, n))
            sp.dma_start(gates_sb[:, :], gates).then_inc(gates_in, 16)

            jobs = ((q_parts, q_scratch, q_stack, Q_RUNS, q1_ready, q_low_ready, q_scratch_out),
                    (k_parts, k_scratch, k_stack, K_RUNS, k1_ready, k_low_ready, k_scratch_out))

            def write_scratch(p):
                for parts, scratch, _, runs, high, low, written in jobs:
                    hold(sp, high, count(p, 1, 1))
                    hold(sp, low, count(p, 2, 2))
                    if not p.early:
                        hold(sp, stack_in[p.par][1], 16 * STACK_DMAS * p.turn)
                    t0 = 0
                    for part, n, copies in runs:
                        src = parts[:, part:part + n, :]
                        if copies > 1:
                            src = src.to_broadcast([P, copies, parts.shape[2]])
                        t1 = t0 + n * copies
                        dst = scratch[p.par, t0:t1].rearrange("t j d i n -> (j d i) t n")
                        sp.dma_start(dst, src).then_inc(written, 16)
                        t0 = t1

            def read_stacks(p, half):
                if p.early:
                    sp.wait_ge(stack_ones, 2)
                else:
                    hold(sp, st_mm, count(p, 2 * UNITS, -4 * UNITS + UNITS * (half + 1)))
                pairs = slice(half * HALF, (half + 1) * HALF)
                for _, scratch, rows, _, _, _, written in jobs:
                    hold(sp, written, count(p, 16 * SCRATCH_DMAS, 16 * SCRATCH_DMAS))
                    for j in range(2):
                        sp.dma_start(rows[p.par][64 * j:64 * j + QK_ROWS, pairs, :], scratch[p.par, :, j, :, pairs, :]
                                     ).then_inc(stack_in[p.par][half], 16)

            def max_rows(a, half):
                hold(sp, neg_maxT_ready, count(a, 2, half + 1))
                if not a.early:
                    hold(sp, neg_max_in[a.par][half], 16 * MAX_DMAS * a.turn)
                sp.dma_start(max_scratch[a.par, half], neg_maxT[:, :]).then_inc(max_scratch_out, 16)
                hold(sp, max_scratch_out, count(a, 32, 16 * (half + 1)))
                rows = max_scratch[a.par, half].rearrange("(m j i) n -> j m i n", j=2, i=HALF)
                for j in range(2):
                    r0 = 64 * j + QK_ROWS
                    sp.dma_start(q_stack[a.par][r0:r0 + M_ROWS, half * HALF:(half + 1) * HALF, :], rows[j]
                                 ).then_inc(neg_max_in[a.par][half], 16)

            def store(d):
                hold(sp, out_ready, count(d, 1, 1))
                sp.dma_start(out[bass.ds(d.n, 1)].rearrange("b (t p) d -> p (b t) d", p=P), x_all[:, d.tiles(), :]
                             ).then_inc(out_done, 16)

            def step(p, a, b, c, d):
                if p and not p.early:
                    load_ctx(p)
                if b:
                    max_rows(b, 1)
                if a and not a.first:
                    read_stacks(a, 1)
                if p and not p.early:
                    load_mask(p)
                if p:
                    write_scratch(p)
                    read_stacks(p, 0)
                if p and p.first:
                    read_stacks(p, 1)
                if a:
                    max_rows(a, 0)
                if d:
                    store(d)

            first_steps(step)
            sp.dma_start(x_all[:, 2 * QT:, :], x_tiles[:, 2 * QT:, :]).then_inc(x_rest_in, 16)
            for dst, src in ((wo_sb[:, :], woT), (wg_sb[:, :], wg), (w1_sb[:, :, :], w1), (b1_sb[:, :, :], b1),
                             (w2_sb[:, :, :, :], w2), (b2_sb[:, :], b2)):
                sp.dma_start(dst, src).then_inc(ffn_in, 16)
            later_steps(sp, step)
            sp.wait_ge(out_done, 16 * B)

        @block.gpsimd
        def _(gp):
            gp.memset(minus_half[:, :], -0.5).then_inc(half_set, 1)
            gp.wait_ge(half_set, 1)

            def constants():
                for p in range(2):
                    gp.memset(k_stack[p][:, :, :].rearrange("p i n -> p (i n)").bitcast(F32), TWO_ONES
                              ).then_inc(stack_ones, 1)
                gp.wait_ge(eye_in, 16)
                gp.tensor_copy(eye_b[:, :], eye_f[:, :]).then_inc(eye_b_set, 1)
                gp.iota(expert_no[:, :, :], pattern=[[0, QT], [1, E]], base=0, channel_multiplier=0,
                        allow_small_or_imprecise_dtypes=True).then_inc(numbers_set, 1)

            def low_parts(a, parts, rest, rest_ready, low_ready, written):
                gp.wait_ge(rest_ready, count(a, 1, 1))
                if not a.first:
                    hold(gp, written, count(a, 16 * SCRATCH_DMAS, 0))
                gp.tensor_scalar(parts[:, 1, :], rest[:, :], 1.0, 1.0, ALU.mult, ALU.mult).then_inc(low_ready, 1)
                gp.wait_ge(low_ready, count(a, 2, 1))
                gp.tensor_tensor(parts[:, 2, :], rest[:, :], parts[:, 1, :], ALU.subtract).then_inc(low_ready, 1)

            def rstd(n, step_sem, dst, ready):
                hold(gp, step_sem, count(n, 5, 5))
                gp.tensor_tensor(dst[:, :], var_eps[:, :], minus_half[:, :], ALU.pow).then_inc(ready, 1)

            def mask_bias(a):
                if not a.early:
                    gp.wait_ge(st_mm, count(a, 2 * UNITS, -2 * UNITS))
                hold(gp, batch_mask_in[a.par], 16 * (a.turn + 1))
                gp.tensor_scalar(maskb[a.par][:, :, :], mask_sb[a.par][:, :, :], MASKED, 1.0, ALU.mult, ALU.mult
                                 ).then_inc(maskb_ready, 1)

            def step(p, a, b, c, d):
                if p:
                    rstd(p, ln1_step, rstd1, rstd1_ready)
                if p and p.first:
                    constants()
                if a:
                    mask_bias(a)
                if p:
                    low_parts(p, q_parts, q_rest, q_rest_ready, q_low_ready, q_scratch_out)
                if c:
                    rstd(c, ln2_step, rstd2, rstd2_ready)
                if p:
                    low_parts(p, k_parts, k_rest, k_rest_ready, k_low_ready, k_scratch_out)

            first_steps(step)
            later_steps(gp, step)

        @block.tensor
        def _(pe):
            def transpose_x(p, b):
                pe.wait_ge(xn_ready, count(p, 1, 1))
                if p.first:
                    pe.wait_ge(eye_in, 16)
                if b:
                    pe.wait_ge(neg_maxT_ready, count(b, 2, 2))
                elif not p.first:
                    pe.wait_ge(k_rest_ready, count(p, 1, 0))
                for t in range(QT):
                    mm = pe.transpose(misc[:, t * P:(t + 1) * P], xn[:, t, :], eye_f[:, :])
                mm.then_inc(xnT_mm, 1)

            def project_q(p):
                pe.wait_ge(xnT_ready, count(p, 1, 1))
                if p.first:
                    pe.wait_ge(wq_in, 16)
                pe.matmul(misc[:, 0:S], wq_sb[:, :], xnT[:, :], start=True, stop=True).then_inc(q_mm, 1)

            def project_k(p, c):
                pe.wait_ge(ctx_in[p.par], 16 * (p.turn + 1))
                if p.first:
                    pe.wait_ge(wk_in, 16)
                pe.wait_ge(q_rest_ready, count(p, 1, 1))
                if c:
                    pe.wait_ge(att_n_ready, count(c, 2, 2))
                pe.matmul(misc[:, :], wk_sb[:, :], ctx_sb[p.par][:, :], start=True, stop=True).then_inc(k_mm, 1)

            def project_v(a, p, c):
                if a.first:
                    pe.wait_ge(wv_in, 16)
                if c:
                    pe.wait_ge(att_nT_ready, count(c, 1, 1))
                elif p:
                    pe.wait_ge(k_rest_ready, count(p, 1, 1))
                for ch in range(KC):
                    mm = pe.matmul(misc[:, ch * P:(ch + 1) * P], ctx_sb[a.par][:, ch * P:(ch + 1) * P], wv_sb[:, :],
                                   start=True, stop=True)
                mm.then_inc(v_mm, 1)

            def max_scores(a, v, masked, spare):
                i, qt = MX_UNITS[v]
                if v % (UNITS // 2) == 0:
                    pe.wait_ge(stack_in[a.par][v // (UNITS // 2)], 16 * STACK_DMAS * (a.turn + 1))
                if v == 0:
                    if masked:
                        pe.wait_ge(eye_b_set, 1)
                        pe.wait_ge(maskb_ready, count(a, 1, 1))
                target = ffn_bank if spare and v % 2 else mx_bank
                if spare:
                    if not (a.first and v < 2):
                        pe.wait_ge(mx_read, count(a, UNITS, v - 1))
                else:
                    pe.wait_ge(mx_read, count(a, UNITS, v))
                for j in range(2):
                    r0 = 64 * j
                    mm = pe.matmul(target[:, j, :], q_stack[a.par][r0:r0 + QK_ROWS, i, qt * P:(qt + 1) * P],
                                   k_stack[a.par][r0:r0 + QK_ROWS, i, :], start=True, stop=not masked)
                if masked:
                    for j in range(2):
                        mm = pe.matmul(target[:, j, :], eye_b[:, :], maskb[a.par][:, qt, :], start=False, stop=True)
                mm.then_inc(mx_mm, 1)

            def keep_clock_up(products, bank_x):
                for _ in range(products):
                    pe.matmul(bank_x[:, 0:P], eye_f[:, :], eye_f[:, :], start=True, stop=True)

            def transpose_max(n, half, c, d):
                pe.wait_ge(neg_max_step, count(n, 6, 3 * (half + 1)))
                if half == 0:
                    pe.wait_ge(eye_b_set, 1)
                    if c:
                        pe.wait_ge(x2_ready, count(c, 1, 1))
                    else:
                        pe.wait_ge(v_ready, count(n, 1, 1))
                elif d:
                    pe.wait_ge(acc_set, count(d, 1, 1))
                elif c:
                    pe.wait_ge(att_n_ready, count(c, 2, 1))
                out_t = misc[:, :].bitcast(BF16)
                for t in range(QT):
                    mm = pe.transpose(out_t[0:M_ROWS * 2 * HALF, t * P:(t + 1) * P],
                                      neg_max_parts[:, t, :, :].rearrange("p m h -> p (m h)"), eye_b[:, :])
                mm.then_inc(neg_max_mm, 1)

            def scores(b, u, masked):
                i, half = divmod(u, 2)
                if u % (UNITS // 2) == 0:
                    pe.wait_ge(neg_max_in[b.par][u // (UNITS // 2)], 16 * MAX_DMAS * (b.turn + 1))
                if not (b.first and u == 0):
                    pe.wait_ge(probs_ready, count(b, 2 * UNITS, 2 * u))
                if b.first and u >= 4:
                    keep_clock_up(1, st_bank[:, 0, :])
                for cc in range(2):
                    for j in range(2):
                        r0, ch = 64 * j, 2 * half + cc
                        rows = QK_ROWS + M_ROWS
                        mm = pe.matmul(st_bank[:, j, cc * S:(cc + 1) * S],
                                       k_stack[b.par][r0:r0 + rows, i, ch * P:(ch + 1) * P],
                                       q_stack[b.par][r0:r0 + rows, i, :], start=True, stop=True, skip_group_check=masked)
                        if masked:
                            for t in range(QT):
                                mm = pe.matmul(st_bank[:, j, cc * S + t * P:cc * S + (t + 1) * P],
                                               maskb[b.par][:, t, ch * P:(ch + 1) * P], eye_b[:, :],
                                               start=False, stop=True, skip_group_check=True)
                        if cc == 1:
                            mm.then_inc(st_mm, 1)

            def values(b, g, ch):
                if ch == 0:
                    pe.wait_ge(probs_ready, count(b, 2 * UNITS, 8 * (g + 1)))
                    if g == 0:
                        pe.wait_ge(v_ready, count(b, 1, 1))
                    if g % 2 == 0 and not (b.first and g == 0):
                        pe.wait_ge(att_ready, count(b, 2, g // 2))
                for jj in range(4):
                    unit = 2 * (jj // 2) + ch // 2
                    cc = ch % 2
                    mm = pe.matmul(av_bank[VW * jj:VW * (jj + 1), (g % 2) * S:(g % 2 + 1) * S],
                                   v_sb[b.par][:, ch, 4 * g + jj, :],
                                   probs[:, g % 2, unit, jj % 2, cc * S:(cc + 1) * S],
                                   start=(ch == 0), stop=(ch == KC - 1), skip_group_check=True)
                if ch == KC - 1:
                    mm.then_inc(av_mm, 1)

            def transpose_heads(n, hh, p, a, b, c, d):
                pe.wait_ge(att_ready, count(n, 2, hh + 1))
                if hh == 1:
                    if p:
                        pe.wait_ge(q_rest_ready, count(p, 1, 1))
                    elif b:
                        pe.wait_ge(neg_maxT_ready, count(b, 2, 2))
                    elif d:
                        pe.wait_ge(acc_set, count(d, 1, 1))
                else:
                    if c:
                        pe.wait_ge(logits_read, count(c, 1, 1))
                    elif a:
                        pe.wait_ge(neg_maxT_ready, count(a, 2, 1))
                for t in range(QT):
                    for gl in range(2):
                        k = 2 * t + gl
                        mm = pe.transpose(misc[:, k * P:(k + 1) * P], att_sb[:, gl, t * P:(t + 1) * P], eye_f[:, :])
                mm.then_inc(attT_mm, 1)

            def transpose_normed(c, p):
                pe.wait_ge(att_n_ready, count(c, 2, 2))
                if p:
                    pe.wait_ge(k_rest_ready, count(p, 1, 1))
                for t in range(QT):
                    mm = pe.transpose(misc[:, t * P:(t + 1) * P], att_n[:, t, :], eye_f[:, :])
                mm.then_inc(att_nT_mm, 1)

            def project_out(c, a):
                pe.wait_ge(att_nT_ready, count(c, 1, 1))
                if c.first:
                    pe.wait_ge(ffn_in, 16 * 6)
                if a:
                    pe.wait_ge(v_ready, count(a, 1, 1))
                for t in range(QT):
                    mm = pe.matmul(misc[:, t * P:(t + 1) * P], att_nT[:, t * P:(t + 1) * P], wo_sb[:, :],
                                   start=True, stop=True)
                mm.then_inc(proj_mm, 1)

            def transpose_x2(c, a):
                pe.wait_ge(xn2_ready, count(c, 1, 1))
                if a:
                    pe.wait_ge(neg_maxT_ready, count(a, 2, 1))
                for t in range(QT):
                    mm = pe.transpose(misc[:, t * P:(t + 1) * P], xn2[:, t, :], eye_f[:, :])
                mm.then_inc(xn2T_mm, 1)

            def gate(c):
                pe.wait_ge(xn2T_ready, count(c, 1, 1))
                for t in range(QT):
                    mm = pe.matmul(misc[:, t * E:(t + 1) * E], xn2T[c.par][:, t * P:(t + 1) * P], wg_sb[:, :],
                                   start=True, stop=True)
                mm.then_inc(logits_mm, 1)

            def transpose_route(c, b):
                pe.wait_ge(route_ready, count(c, 1, 1))
                if b:
                    pe.wait_ge(att_n_ready, count(b, 2, 1))
                for t in range(QT):
                    mm = pe.transpose(misc[0:E, t * P:(t + 1) * P], route_w[c.par][:, t, :], eye_f[:, :])
                mm.then_inc(routeT_mm, 1)

            def bias2(c):
                pe.wait_ge(routeT_ready, count(c, 1, 1))
                for t in range(QT):
                    mm = pe.matmul(misc[:, t * P:(t + 1) * P], route_wT[:, t * P:(t + 1) * P], b2_sb[:, :],
                                   start=True, stop=True)
                mm.then_inc(b2_mm, 1)

            def hidden(n, x_, spare):
                if x_ == 0:
                    pe.wait_ge(xn2T_ready, count(n, 1, 1))
                if spare:
                    bank_x = mx_bank[:, x_ % 2, :]
                    pe.wait_ge(mx_read, B * UNITS)
                    pe.wait_ge(h_ready, count(n, 2 * E, 2 * x_ - 2))
                else:
                    bank_x = h_bank
                    if not (n.first and x_ == 0):
                        pe.wait_ge(h_ready, count(n, 2 * E, 2 * x_))
                for ch in range(HC):
                    mm = pe.matmul(bank_x[:, ch * S:(ch + 1) * S], w1_sb[:, x_, ch * P:(ch + 1) * P],
                                   xn2T[n.par][:, :], start=True, stop=True)
                mm.then_inc(h_mm, 1)

            def expert_out(n, x_):
                pe.wait_ge(h_ready, count(n, 2 * E, 2 * x_ + 2))
                el = x_ % 2
                if el == 0 and not (n.first and x_ == 0):
                    pe.wait_ge(acc_step, count(n, 2 * E, 2 * x_))
                for t in range(QT):
                    k = 2 * el + t
                    for ch in range(HC):
                        mm = pe.matmul(y_bank[:, k * P:(k + 1) * P], h_sb[:, x_ % 4, ch, t * P:(t + 1) * P],
                                       w2_sb[:, x_, ch, :], start=(ch == 0), stop=(ch == HC - 1))
                mm.then_inc(y_mm, 1)

            def step_of(masked):
                def step(p, a, b, c, d):
                    for slot in range(UNITS):
                        if b:
                            scores(b, slot, masked)
                        if a:
                            max_scores(a, slot, masked, spare=not c)
                        if a and not b:
                            keep_clock_up(2, av_bank)
                        if b and b.first and slot < 4:
                            keep_clock_up(5, av_bank)
                        if c and c.first and slot < 11:
                            keep_clock_up(1, h_bank)
                        if slot < 4 and c:
                            values(c, 3, slot)
                        if slot >= 4 and b:
                            values(b, slot // 4 - 1, slot % 4)
                        if c and slot in HIDDEN_SLOTS:
                            hidden(c, HIDDEN_SLOTS[slot], spare=not a)
                        if d and slot in LATER_HIDDEN_SLOTS:
                            hidden(d, LATER_HIDDEN_SLOTS[slot], spare=not a)
                        if c and slot in OUT_SLOTS:
                            expert_out(c, OUT_SLOTS[slot])
                        if d and slot in LATER_OUT_SLOTS:
                            expert_out(d, LATER_OUT_SLOTS[slot])
                        if b and slot == 0:
                            transpose_max(b, 1, c, d)
                        if p and slot == 1:
                            transpose_x(p, b)
                        if p and slot == 3:
                            project_q(p)
                        if c and slot == 4:
                            transpose_heads(c, 1, p, a, b, None, d)
                        if p and slot == 5:
                            project_k(p, c)
                        if c and slot == 6:
                            transpose_normed(c, p)
                        if a and slot == 7:
                            project_v(a, p, c)
                        if c and slot == 8:
                            project_out(c, a)
                        if a and slot == 9:
                            transpose_max(a, 0, c, None)
                        if c and slot == 10:
                            transpose_x2(c, a)
                        if c and slot == 11:
                            gate(c)
                        if b and slot == 12:
                            transpose_heads(b, 0, None, a, None, c, None)
                        if c and slot == 14:
                            transpose_route(c, b)
                        if c and slot == 15:
                            bias2(c)
                return step

            first_steps(step_of(False))
            keep_clock_up(8, av_bank)
            pe.wait_ge(any_col_set, 1)
            pe.wait_ge(k_rest_ready, 2)
            pe.transpose(misc[0:1, 0:P], any_col[:, :], eye_f[:, :]).then_inc(any_mm, 1)
            pe.wait_ge(any_flag_set, 1)
            keep_clock_up(6, av_bank)
            any_masked = pe.value_load(any_flag[0:1, 0:1])
            with pe.If(any_masked > 0):
                later_steps(pe, step_of(True))
            with pe.Else():
                later_steps(pe, step_of(False))

        @block.scalar
        def _(act):
            def copy_xnT(a):
                act.wait_ge(xnT_mm, count(a, 1, 1))
                act.copy(xnT[:, :], misc[:, 0:S]).then_inc(xnT_ready, 1)

            def high_part(a, mm, written, parts, width, ready):
                act.wait_ge(mm, count(a, 1, 1))
                if not a.first:
                    act.wait_ge(written, count(a, 16 * SCRATCH_DMAS, 0))
                act.copy(parts[:, 0, :], misc[:, 0:width]).then_inc(ready, 1)

            def copy_v(a):
                act.wait_ge(v_mm, count(a, 1, 1))
                if a.first:
                    act.wait_ge(v_filled, 4)
                if not a.early:
                    act.wait_ge(av_mm, count(a, 4, -4))
                act.copy(v_sb[a.par][:, :, :, 0:DK].rearrange("p c h d -> p (c h) d"),
                         misc[:, :].rearrange("p (c d) -> p c d", d=DK)).then_inc(v_ready, 1)

            def exps(b, u):
                g = u // 4
                for j in range(2):
                    act.wait_ge(st_mm, count(b, 2 * UNITS, 2 * u + j + 1))
                    if j == 0 and u % 4 == 0 and not (b.first and g < 2):
                        act.wait_ge(av_mm, count(b, 4, g - 1))
                    act.activation(probs[:, g % 2, u % 4, j, :], st_bank[:, j, :], ACT.Exp, scale=SCALE
                                   ).then_inc(probs_ready, 1)

            def copy_heads(b, hh):
                act.wait_ge(av_mm, count(b, 4, 2 * hh + 2))
                if not (b.first and hh == 0):
                    act.wait_ge(attT_mm, count(b, 2, hh))
                act.copy(att_sb[:, :, :].rearrange("p g s -> p (g s)"), av_bank[:, :]).then_inc(att_ready, 1)

            def copy_normed(c):
                act.wait_ge(att_nT_mm, count(c, 1, 1))
                act.copy(att_nT[:, :], misc[:, 0:S]).then_inc(att_nT_ready, 1)

            def copy_x2T(c):
                act.wait_ge(xn2T_mm, count(c, 1, 1))
                act.copy(xn2T[c.par][:, :], misc[:, 0:S]).then_inc(xn2T_ready, 1)

            def route_exp(c):
                act.wait_ge(logits_read, count(c, 1, 1))
                act.activation(expert_e[:, :, :], logit_d[:, :, :], ACT.Exp).then_inc(expert_e_ready, 1)

            def copy_routeT(c):
                act.wait_ge(routeT_mm, count(c, 1, 1))
                act.copy(route_wT[:, :], misc[0:E, 0:S]).then_inc(routeT_ready, 1)

            def set_acc(c):
                act.wait_ge(b2_mm, count(c, 1, 1))
                act.copy(acc[c.par][:, :, :].rearrange("p t d -> p (t d)"), misc[:, 0:S]).then_inc(acc_set, 1)

            def relu(n, x_, spare):
                bank_x = mx_bank[:, x_ % 2, :] if spare else h_bank
                if not (n.first and x_ < 4):
                    act.wait_ge(y_mm, count(n, E, x_ - 3))
                if n.first and x_ == 0:
                    act.wait_ge(ffn_in, 16 * 6)
                act.wait_ge(h_mm, count(n, E, x_ + 1))
                for ch in range(HC):
                    act.activation(h_sb[:, x_ % 4, ch, :], bank_x[:, ch * S:(ch + 1) * S], ACT.Relu,
                                   bias=b1_sb[:, x_, ch:ch + 1]).then_inc(h_ready, 1)

            def step(p, a, b, c, d):
                for slot in range(UNITS):
                    if b:
                        exps(b, slot)
                    if c and slot == 3:
                        copy_heads(c, 1)
                    if b and slot == 11:
                        copy_heads(b, 0)
                    if c and slot in HIDDEN_SLOTS:
                        relu(c, HIDDEN_SLOTS[slot], spare=not a)
                    if d and slot in LATER_HIDDEN_SLOTS:
                        relu(d, LATER_HIDDEN_SLOTS[slot], spare=not a)
                    if p and slot == 1:
                        copy_xnT(p)
                    if p and slot == 3:
                        high_part(p, q_mm, q_scratch_out, q_parts, S, q1_ready)
                    if p and slot == 5:
                        high_part(p, k_mm, k_scratch_out, k_parts, S2, k1_ready)
                    if c and slot == 6:
                        copy_normed(c)
                    if a and slot == 7:
                        copy_v(a)
                    if c and slot == 10:
                        copy_x2T(c)
                    if c and slot == 12:
                        route_exp(c)
                    if c and slot == 14:
                        copy_routeT(c)
                    if c and slot == 15:
                        set_acc(c)

            first_steps(step)
            act.wait_ge(gates_in, 16)
            act.activation(gate_t[:, :], gates_sb[:, :], ACT.Tanh).then_inc(gates_set, 1)
            later_steps(act, step)

        @block.vector
        def _(dve):
            def statistics(n, step_sem):
                if n.third:
                    hold(dve, x_rest_in, 16)
                for t in range(QT):
                    dve.bn_stats(ln_stats[:, t, :], x_all[:, bass.ds(2 * n.n + t, 1), :].rearrange("p t d -> p (t d)")
                                 ).then_inc(step_sem, 1)
                hold(dve, step_sem, count(n, 5, 2))
                for t in range(QT):
                    dve.bn_aggr(ln_mv[:, t, :], ln_stats[:, t, :]).then_inc(step_sem, 1)
                dve.wait_ge(step_sem, count(n, 5, 4))
                dve.tensor_scalar(var_eps[:, :], ln_mv[:, :, 1], EPS, None, ALU.add).then_inc(step_sem, 1)

            def layernorm(n, rstd_ready, rstd, dst, dst_free, ready):
                dve.wait_ge(rstd_ready, count(n, 1, 1))
                if not n.first:
                    dve.wait_ge(dst_free, count(n, 1, 0))
                for t in range(QT):
                    ln = dve.tensor_scalar(dst[:, t, :], x_all[:, bass.ds(2 * n.n + t, 1), :].rearrange("p t d -> p (t d)"),
                                           ln_mv[:, t, 0:1], rstd[:, t:t + 1], ALU.subtract, ALU.mult)
                ln.then_inc(ready, 1)

            def rest(a, high, parts, dst, width, low, ready):
                dve.wait_ge(high, count(a, 1, 1))
                if not a.first:
                    dve.wait_ge(low, count(a, 2, 0))
                dve.tensor_tensor(dst[:, :], misc[:, 0:width], parts[:, 0, :], ALU.subtract).then_inc(ready, 1)

            def reduce_max(a, v, spare):
                i, qt = MX_UNITS[v]
                source = ffn_bank if spare and v % 2 else mx_bank
                dve.wait_ge(mx_mm, count(a, UNITS, v + 1))
                dve.tensor_reduce(row_max[:, qt, :, i], source[:, :, :], AX_X, ALU.max).then_inc(mx_read, 1)

            def negate_max(a, half):
                dve.wait_ge(mx_read, count(a, UNITS, UNITS // 2 * (half + 1)))
                pairs = slice(half * HALF, (half + 1) * HALF)
                dve.tensor_scalar(neg_max[:, :, :, :], row_max[:, :, :, pairs], LOWEST, -1.0, ALU.max, ALU.mult
                                  ).then_inc(neg_max_step, 1)
                dve.wait_ge(neg_max_step, count(a, 6, 3 * half + 1))
                if not (a.first and half == 0):
                    dve.wait_ge(neg_max_mm, count(a, 2, half))
                src = neg_max[:, :, :, :].rearrange("p t j i -> p t (j i)")
                dve.tensor_copy(neg_max_parts[:, :, 0, :], src).then_inc(neg_max_step, 1)
                dve.wait_ge(neg_max_step, count(a, 6, 3 * half + 2))
                dve.tensor_tensor(neg_max_parts[:, :, 1, :], src, neg_max_parts[:, :, 0, :], ALU.subtract
                                  ).then_inc(neg_max_step, 1)

            def copy_maxT(n, half):
                dve.wait_ge(neg_max_mm, count(n, 2, half + 1))
                if not (n.first and half == 0):
                    dve.wait_ge(max_scratch_out, count(n, 32, 16 * half))
                dve.tensor_copy(neg_maxT[:, :], misc[:, :].bitcast(BF16)[0:M_ROWS * 2 * HALF, 0:S]
                                ).then_inc(neg_maxT_ready, 1)

            def normalise(b, hh):
                dve.wait_ge(attT_mm, count(b, 2, hh + 1))
                heads = misc[:, :].rearrange("p (k w) -> p k w", w=VW)
                dve.tensor_scalar(den[:, :], heads[:, :, DK], 1e-30, None, ALU.max).then_inc(den_step, 1)
                dve.wait_ge(den_step, count(b, 4, 2 * hh + 1))
                dve.reciprocal(rden[:, :], den[:, :]).then_inc(den_step, 1)
                dve.wait_ge(den_step, count(b, 4, 2 * hh + 2))
                if hh == 0 and not b.first:
                    dve.wait_ge(att_nT_mm, count(b, 1, 0))
                half = H // 2
                dve.tensor_tensor(
                    att_n[:, :, hh * 64:(hh + 1) * 64].rearrange("p t (h d) -> p t h d", d=DK),
                    misc[:, :].rearrange("p (t h w) -> p t h w", t=QT, h=half)[:, :, :, 0:DK],
                    rden[:, :].rearrange("p (t h) -> p t h", t=QT).unsqueeze(3).to_broadcast([P, QT, half, DK]),
                    ALU.mult).then_inc(att_n_ready, 1)

            def residual(c):
                dve.wait_ge(proj_mm, count(c, 1, 1))
                if c.first:
                    dve.wait_ge(gates_set, 1)
                xt = x_all[:, c.tiles(), :]
                dve.scalar_tensor_tensor(out=xt, in0=misc[:, 0:S].rearrange("p (t d) -> p t d", t=QT),
                                         scalar=gate_t[:, 0:1], in1=xt, op0=ALU.mult, op1=ALU.add).then_inc(x2_ready, 1)
                hold(dve, x2_ready, count(c, 1, 1))

            def logits(c):
                hold(dve, logits_mm, count(c, 1, 1))
                lg = misc[:, 0:QT * E].rearrange("p (t e) -> p t e", t=QT)
                for t in range(QT):
                    dve.max(logit_top[:, t, :], lg[:, t, :]).then_inc(logits_step, 1)
                dve.wait_ge(logits_step, count(c, 2, 2))
                dve.tensor_tensor(logit_d[:, :, :], lg, logit_top[:, :, 0:1].to_broadcast([P, QT, E]), ALU.subtract
                                  ).then_inc(logits_read, 1)

            def routed(c, k, ins):
                ins.then_inc(route_step, 1)
                return count(c, ROUTE_STEPS, k)

            def route_softmax(c):
                dve.wait_ge(expert_e_ready, count(c, 1, 1))
                done = routed(c, 1, dve.tensor_reduce(expert_sum[:, :], expert_e[:, :, :], AX_X, ALU.add))
                dve.wait_ge(route_step, done)
                done = routed(c, 2, dve.reciprocal(expert_inv[:, :], expert_sum[:, :]))
                dve.wait_ge(route_step, done)
                done = routed(c, 3, dve.tensor_tensor(
                    expert_p[:, :, :], expert_e[:, :, :],
                    expert_inv[:, :].unsqueeze(2).to_broadcast([P, QT, E]), ALU.mult))
                hold(dve, route_step, done)
                for t in range(QT):
                    top = dve.max(top_p[:, t, :], expert_p[:, t, :])
                done = routed(c, 4, top)
                hold(dve, route_step, done)
                for t in range(QT):
                    top = dve.max_index(top_i[:, t, :], top_p[:, t, :], expert_p[:, t, :])
                routed(c, 5, top)

            def route_choose(c):
                dve.wait_ge(route_step, count(c, ROUTE_STEPS, 5))
                done = routed(c, 6, dve.tensor_copy(top_f[:, :, :], top_i[:, :, 0:2]))
                dve.wait_ge(route_step, done)
                for m in range(2):
                    done = routed(c, 7 + m, dve.tensor_tensor(
                        is_top[:, m, :, :], expert_no[:, :, :],
                        top_f[:, :, m:m + 1].to_broadcast([P, QT, E]), ALU.is_equal))
                dve.wait_ge(route_step, done)
                done = routed(c, 9, dve.tensor_tensor(chosen[:, :, :], is_top[:, 0, :, :], is_top[:, 1, :, :], ALU.add))
                dve.wait_ge(route_step, done)
                dve.tensor_tensor(route_w[c.par][:, :, :], chosen[:, :, :], expert_p[:, :, :], ALU.mult
                                  ).then_inc(route_ready, 1)

            def add_experts(c, p):
                dve.wait_ge(y_mm, count(c, E, 2 * p + 2))
                for el in range(2):
                    x_ = 2 * p + el
                    if x_ == 0:
                        dve.wait_ge(acc_set, count(c, 1, 1))
                        dve.wait_ge(route_ready, count(c, 1, 1))
                    else:
                        dve.wait_ge(acc_step, count(c, 2 * E, 2 * x_))
                    for t in range(QT):
                        k = 2 * el + t
                        dve.scalar_tensor_tensor(out=acc[c.par][:, t, :], in0=y_bank[:, k * P:(k + 1) * P],
                                                 scalar=route_w[c.par][:, t, x_:x_ + 1], in1=acc[c.par][:, t, :],
                                                 op0=ALU.mult, op1=ALU.add).then_inc(acc_step, 1)

            def finish(d):
                dve.wait_ge(acc_step, count(d, 2 * E, 2 * E))
                xt = x_all[:, d.tiles(), :]
                dve.scalar_tensor_tensor(out=xt, in0=acc[d.par][:, :, :], scalar=gate_t[:, 1:2], in1=xt,
                                         op0=ALU.mult, op1=ALU.add).then_inc(out_ready, 1)

            def fill_values(q):
                dve.memset(v_sb[q][:, :, :, :], 0.0).then_inc(v_filled, 1)
                dve.wait_ge(v_filled, 2 * q + 1)
                dve.memset(v_sb[q][:, :, :, DK:DK + 1], 1.0).then_inc(v_filled, 1)

            def step(p, a, b, c, d):
                for slot in range(UNITS):
                    if p and slot == 0:
                        statistics(p, ln1_step)
                    if p and slot == 1:
                        layernorm(p, rstd1_ready, rstd1, xn, xnT_mm, xn_ready)
                    if p and p.first and slot in (1, 4):
                        fill_values(slot // 4)
                    if a:
                        reduce_max(a, slot, spare=not c)
                    if b and slot == 0:
                        copy_maxT(b, 1)
                    if d and slot in ADD_SLOTS:
                        add_experts(d, ADD_SLOTS[slot])
                    if p and slot == 3:
                        rest(p, q1_ready, q_parts, q_rest, S, q_low_ready, q_rest_ready)
                    if c and slot == 4:
                        normalise(c, 1)
                    if p and slot == 5:
                        rest(p, k1_ready, k_parts, k_rest, S2, k_low_ready, k_rest_ready)
                    if a and slot == 7:
                        negate_max(a, 0)
                    if c and slot == 8:
                        residual(c)
                        statistics(c, ln2_step)
                    if a and slot == 9:
                        copy_maxT(a, 0)
                    if c and slot == 9:
                        layernorm(c, rstd2_ready, rstd2, xn2, xn2T_mm, xn2_ready)
                    if c and slot == 11:
                        logits(c)
                    if b and slot == 12:
                        normalise(b, 0)
                    if c and slot == 12:
                        route_softmax(c)
                    if c and slot == 13:
                        route_choose(c)
                    if d and slot == 14:
                        finish(d)
                    if a and slot == 15:
                        negate_max(a, 1)

            dve.wait_ge(x_in, 16)
            first_steps(step, between=lambda: dve.wait_ge(x_second_in, 16))
            dve.wait_ge(mask_in, 16)
            dve.tensor_reduce(any_col[:, :], mask_all[:, :, :].rearrange("p t k -> p (t k)").bitcast(I32), AX_X, ALU.max
                              ).then_inc(any_col_set, 1)
            dve.wait_ge(any_mm, 1)
            dve.tensor_reduce(any_row[:, :], misc[0:1, 0:P], AX_X, ALU.max).then_inc(any_row_set, 1)
            dve.wait_ge(any_row_set, 1)
            dve.tensor_scalar(any_flag[:, :], any_row[:, :], 1.0, None, ALU.min).then_inc(any_flag_set, 1)
            dve.wait_ge(numbers_set, 1)
            later_steps(dve, step)


def kernel(x, ctx_1024, mask_BxSxS2_bf0, g_xattn, g_ffn, L0_xattn_W_Q, L0_xattn_W_K, L0_xattn_W_V, L0_xattn_W_O,
           L0_ffn_Wg, L0_ffn_W1, L0_ffn_b1, L0_ffn_W2, L0_ffn_b2):
    import numpy as np
    import concourse.bacc as bacc
    from concourse.bass_utils import run_bass_kernel_spmd

    def pair_order(w):
        return np.ascontiguousarray(np.asarray(w).T.reshape(D, PAIRS, 2, DK).transpose(0, 2, 3, 1).reshape(D, D))

    arrays = {
        "x": np.asarray(x),
        "ctxT": np.ascontiguousarray(np.asarray(ctx_1024).transpose(0, 2, 1)),
        "mask": np.asarray(mask_BxSxS2_bf0),
        "gates": np.ascontiguousarray(np.broadcast_to(
            np.concatenate([np.asarray(g_xattn), np.asarray(g_ffn)])[None, :], (P, 2))),
        "wqT": pair_order(L0_xattn_W_Q),
        "wkT": pair_order(L0_xattn_W_K),
        "wvT": np.ascontiguousarray(np.asarray(L0_xattn_W_V).T),
        "woT": np.ascontiguousarray(np.asarray(L0_xattn_W_O).T),
        "wg": np.asarray(L0_ffn_Wg),
        "w1": np.ascontiguousarray(np.asarray(L0_ffn_W1).transpose(1, 0, 2)),
        "b1": np.ascontiguousarray(np.asarray(L0_ffn_b1).reshape(E, HC, P).transpose(2, 0, 1)),
        "w2": np.ascontiguousarray(np.asarray(L0_ffn_W2).reshape(E, HC, P, D).transpose(2, 0, 1, 3)),
        "b2": np.asarray(L0_ffn_b2),
        "eye": np.eye(P, dtype=np.float32),
    }
    nc = bacc.Bacc("TRN2", target_bir_lowering=False, num_devices=1)
    args = {name: nc.dram_tensor(f"in_{name}", a.shape, mybir.dt.from_np(a.dtype), kind="ExternalInput").ap()
            for name, a in arrays.items()}
    result = nc.dram_tensor("out_0", (B, S, D), F32, kind="ExternalOutput").ap()
    build(nc, out=result, **args)
    run = run_bass_kernel_spmd(nc, [{f"in_{name}": a for name, a in arrays.items()}], core_ids=[0])
    return run.results[0]["out_0"]
```
